# Optimizing a Trainium2 kernel written in Bass

```python
import numpy as np
import jax
import jax.numpy as jnp

def _softmax(x, axis=-1):
    return jax.nn.softmax(x, axis=axis)

def _gelu(x):
    return jax.nn.gelu(x, approximate=True)

def _silu(x):
    return jax.nn.silu(x)

def _sigmoid(x):
    return jax.nn.sigmoid(x)

def _layernorm(x, axis=-1, eps=1e-05):
    m = jnp.mean(x, axis=axis, keepdims=True)
    v = jnp.var(x, axis=axis, keepdims=True)
    return (x - m) / jnp.sqrt(v + eps)

def _scatter_add(tgt, idx, src, axis=0):
    return tgt.at[idx].add(src)

def _segment_sum(src, seg, n):
    return jax.ops.segment_sum(src, seg, n)
kernel_name = 'mk_recurrent_d1_jaxref_r8_866521'

def setup_inputs(seed: int=0):
    np.random.seed(seed)
    _w = jnp.asarray

    def _L0_attn_setup():
        import jax, jax.numpy as jnp
        import numpy as np
        B, N, C = (32, 64, 128)
        H = 16
        D = C // H
        MAX_SEQ = 64
        BASE = 10000.0

        def _rope_tables(n, d):
            position = jnp.arange(n, dtype=jnp.float32)[:, None]
            div_term = jnp.exp(jnp.arange(0, d, 2, dtype=jnp.float32) * (-np.log(BASE) / d))
            ang = position * div_term
            return (jnp.sin(ang), jnp.cos(ang))

        def _apply_rope(x, sin, cos):
            x1 = x[..., ::2]
            x2 = x[..., 1::2]
            out = jnp.stack([x1 * cos - x2 * sin, x1 * sin + x2 * cos], axis=-1)
            return out.reshape(*x.shape[:-1], -1)
        key = jax.random.key(seed)
        k1, k2, k3, k4, k5 = jax.random.split(key, 5)
        s = 0.02
        return {'x': jax.random.normal(k1, (B, N, C), dtype=jnp.float32), 'w_qkv': jax.random.normal(k2, (3 * C, C), dtype=jnp.float32) * s, 'b_qkv': jax.random.normal(k3, (3 * C,), dtype=jnp.float32) * s, 'w_lepe': jax.random.normal(k4, (C, 1, 3), dtype=jnp.float32) * s, 'b_lepe': jax.random.normal(k5, (C,), dtype=jnp.float32) * s}
    _L0_attn_in = _L0_attn_setup()

    def _L0_ffn_setup():
        import jax, jax.numpy as jnp
        import numpy as np
        B, T, C = (2, 128, 128)
        H = 512
        E_R, E_S, K = (8, 2, 2)

        def _rmsnorm(x, g):
            eps = jnp.finfo(x.dtype).eps
            return x * jax.lax.rsqrt(jnp.mean(x * x, axis=-1, keepdims=True) + eps) * g

        def _experts_mlp(x, g, W1, b1, W2, b2):
            xn = _rmsnorm(x, g)
            h = jnp.einsum('btc,ech->bteh', xn, W1) + b1
            h = jax.nn.gelu(h, approximate=False)
            return jnp.einsum('bteh,ehc->btec', h, W2) + b2
        key = jax.random.key(seed)
        ks = jax.random.split(key, 12)
        s = 0.02
        return {'u': jax.random.normal(ks[0], (B, T, C), dtype=jnp.float32), 'g_shared': jnp.ones((C,), jnp.float32), 'W1_s': jax.random.normal(ks[1], (E_S, C, H), jnp.float32) * s, 'b1_s': jax.random.normal(ks[2], (E_S, H), jnp.float32) * s, 'W2_s': jax.random.normal(ks[3], (E_S, H, C), jnp.float32) * s, 'b2_s': jax.random.normal(ks[4], (E_S, C), jnp.float32) * s, 'g_routed': jnp.ones((C,), jnp.float32), 'W1_r': jax.random.normal(ks[5], (E_R, C, H), jnp.float32) * s, 'b1_r': jax.random.normal(ks[6], (E_R, H), jnp.float32) * s, 'W2_r': jax.random.normal(ks[7], (E_R, H, C), jnp.float32) * s, 'b2_r': jax.random.normal(ks[8], (E_R, C), jnp.float32) * s, 'centroids': jax.random.normal(ks[9], (C, E_R), jnp.float32) * s}
    _L0_ffn_in = _L0_ffn_setup()
    _d = {'L0_attn_x': _L0_attn_in['x'], 'L0_attn_w_qkv': _L0_attn_in['w_qkv'], 'L0_attn_b_qkv': _L0_attn_in['b_qkv'], 'L0_attn_w_lepe': _L0_attn_in['w_lepe'], 'L0_attn_b_lepe': _L0_attn_in['b_lepe'], 'L0_ffn_g_shared': _L0_ffn_in['g_shared'], 'L0_ffn_W1_s': _L0_ffn_in['W1_s'], 'L0_ffn_b1_s': _L0_ffn_in['b1_s'], 'L0_ffn_W2_s': _L0_ffn_in['W2_s'], 'L0_ffn_b2_s': _L0_ffn_in['b2_s'], 'L0_ffn_g_routed': _L0_ffn_in['g_routed'], 'L0_ffn_W1_r': _L0_ffn_in['W1_r'], 'L0_ffn_b1_r': _L0_ffn_in['b1_r'], 'L0_ffn_W2_r': _L0_ffn_in['W2_r'], 'L0_ffn_b2_r': _L0_ffn_in['b2_r'], 'L0_ffn_centroids': _L0_ffn_in['centroids']}
    _x0 = _d['L0_attn_x']
    _d['L0_attn_x'] = jax.random.normal(jax.random.fold_in(jax.random.key(seed), 1), (4, 1024, 128), dtype=_x0.dtype)
    del _x0
    return _d

def reference(L0_attn_x, L0_attn_w_qkv, L0_attn_b_qkv, L0_attn_w_lepe, L0_attn_b_lepe, L0_ffn_g_shared, L0_ffn_W1_s, L0_ffn_b1_s, L0_ffn_W2_s, L0_ffn_b2_s, L0_ffn_g_routed, L0_ffn_W1_r, L0_ffn_b1_r, L0_ffn_W2_r, L0_ffn_b2_r, L0_ffn_centroids):

    def _L0_attn_ref(x, w_qkv, b_qkv, w_lepe, b_lepe):
        import jax, jax.numpy as jnp
        import numpy as np
        B, N, C = (32, 64, 128)
        H = 16
        D = C // H
        MAX_SEQ = 64
        BASE = 10000.0

        def _rope_tables(n, d):
            position = jnp.arange(n, dtype=jnp.float32)[:, None]
            div_term = jnp.exp(jnp.arange(0, d, 2, dtype=jnp.float32) * (-np.log(BASE) / d))
            ang = position * div_term
            return (jnp.sin(ang), jnp.cos(ang))

        def _apply_rope(x, sin, cos):
            x1 = x[..., ::2]
            x2 = x[..., 1::2]
            out = jnp.stack([x1 * cos - x2 * sin, x1 * sin + x2 * cos], axis=-1)
            return out.reshape(*x.shape[:-1], -1)
        b, n, c = x.shape
        scale = 1.0 / np.sqrt(D)
        sin, cos = _rope_tables(n, D)
        qkv = (x @ w_qkv.T + b_qkv).reshape(b, n, 3, H, D).transpose(2, 0, 3, 1, 4)
        q, k, v = (qkv[0], qkv[1], qkv[2])
        q = jax.nn.elu(q) + 1.0
        k = jax.nn.elu(k) + 1.0
        q = _apply_rope(q, sin, cos)
        k = _apply_rope(k, sin, cos)
        attn = jnp.einsum('bhnd,bhmd->bhnm', q, k) * scale
        attn = jax.nn.softmax(attn, axis=-1)
        attn_out = jnp.einsum('bhnm,bhmd->bhnd', attn, v)
        attn_out = attn_out.transpose(0, 2, 1, 3).reshape(b, n, c)
        v_conv = v.transpose(0, 2, 1, 3).reshape(b, n, c).transpose(0, 2, 1)
        lepe = jax.lax.conv_general_dilated(v_conv, w_lepe, window_strides=(1,), padding=((1, 1),), dimension_numbers=('NCH', 'OIH', 'NCH'), feature_group_count=c) + b_lepe[None, :, None]
        lepe = lepe.transpose(0, 2, 1)
        return attn_out + lepe

    def _L0_ffn_ref(u, g_shared, W1_s, b1_s, W2_s, b2_s, g_routed, W1_r, b1_r, W2_r, b2_r, centroids):
        import jax, jax.numpy as jnp
        import numpy as np
        B, T, C = (2, 128, 128)
        H = 512
        E_R, E_S, K = (8, 2, 2)

        def _rmsnorm(x, g):
            eps = jnp.finfo(x.dtype).eps
            return x * jax.lax.rsqrt(jnp.mean(x * x, axis=-1, keepdims=True) + eps) * g

        def _experts_mlp(x, g, W1, b1, W2, b2):
            xn = _rmsnorm(x, g)
            h = jnp.einsum('btc,ech->bteh', xn, W1) + b1
            h = jax.nn.gelu(h, approximate=False)
            return jnp.einsum('bteh,ehc->btec', h, W2) + b2
        h_s = _experts_mlp(u, g_shared, W1_s, b1_s, W2_s, b2_s).sum(axis=-2)
        scores = jax.nn.sigmoid(u @ centroids)
        gpk, i_topk = jax.lax.top_k(scores, K)
        gk = gpk / scores.sum(axis=-1, keepdims=True)
        routed_all = _experts_mlp(u, g_routed, W1_r, b1_r, W2_r, b2_r)
        routed_topk = jnp.take_along_axis(routed_all, i_topk[..., None], axis=2)
        h_r = (gk[..., None] * routed_topk).sum(axis=-2)
        return u + h_s + h_r
    x = L0_attn_x
    xn = _layernorm(x, axis=-1)
    s = _L0_attn_ref(xn, L0_attn_w_qkv, L0_attn_b_qkv, L0_attn_w_lepe, L0_attn_b_lepe)
    g = _silu(_L0_ffn_ref(xn, L0_ffn_g_shared, L0_ffn_W1_s, L0_ffn_b1_s, L0_ffn_W2_s, L0_ffn_b2_s, L0_ffn_g_routed, L0_ffn_W1_r, L0_ffn_b1_r, L0_ffn_W2_r, L0_ffn_b2_r, L0_ffn_centroids))
    x = x + s * g
    return x

_drawn_inputs = setup_inputs


def setup_inputs(seed=0):
    import zlib

    import numpy as np

    out = dict(_drawn_inputs(seed))
    spreads = {'L0_ffn_g_shared': (1.0, 0.6), 'L0_ffn_g_routed': (1.0, 0.6)}
    factors = {'L0_attn_w_qkv': 7.412,
     'L0_attn_b_qkv': 4.515,
     'L0_attn_w_lepe': 8.0,
     'L0_attn_b_lepe': 4.616,
     'L0_ffn_W1_s': 8.0,
     'L0_ffn_b1_s': 8.0,
     'L0_ffn_W2_s': 8.0,
     'L0_ffn_b2_s': 21.422,
     'L0_ffn_W1_r': 8.0,
     'L0_ffn_b1_r': 35.344,
     'L0_ffn_W2_r': 8.0,
     'L0_ffn_b2_r': 64.0,
     'L0_ffn_centroids': 8.0}
    for name, (base, spread) in spreads.items():
        noise = np.random.default_rng([zlib.crc32(name.encode()), seed]).standard_normal(out[name].shape)
        drawn = base * np.exp(spread * noise) if base else spread * noise
        out[name] = jnp.asarray(drawn.astype(out[name].dtype))
    for name, factor in factors.items():
        out[name] = (out[name] * factor).astype(out[name].dtype)
    return out
```

```python
import concourse.bass as bass
from concourse import mybir
from contextlib import ExitStack

P = 128
C = 128
B, T = 4, 1024
NTOK = B * T
TILES = NTOK // P
BT = T // P
H, D = 16, 8
HG, J = 4, 4
GF = J * D
HID = 512
HT = HID // P
ES, ER = 2, 8
E = ES + ER
CH = 512
NCH = NTOK // CH
CT = CH // P
SCALE = float(D) ** -0.5
LN_EPS = 1e-5
RMS_EPS = 1.1920929e-07

F32 = mybir.dt.float32
F32R = mybir.dt.float32r
ALU = mybir.AluOpType
ACT = mybir.ActivationFunctionType
AX = mybir.AxisListType


def wait_apart(eng, sem, value, passed):
    eng.wait_ge(sem, value)
    eng.sem_inc(passed, 1)


class Chain:

    def __init__(self, eng, sem, base=0, passed=None):
        self.eng, self.sem, self.base, self.n, self.passed = eng, sem, base, 0, passed

    def did(self, ins):
        ins.then_inc(self.sem, 1)
        self.n += 1
        return ins

    def settle(self, apart=False):
        self.eng.wait_ge(self.sem, self.base + self.n)
        if apart:
            self.eng.sem_inc(self.passed, 1)


def prologue(nc, keep, ffn, io, psum):
    QT = BT
    STEPS = 4
    with ExitStack() as ctx:
        def sb(name, shape, dt=F32):
            return ctx.enter_context(nc.sbuf_tensor(name, shape, dt))

        def sem(name):
            return ctx.enter_context(nc.semaphore(name))

        x_q = [sb(f"x_q{i}", [P, QT, C]) for i in range(2)]
        xn_q = [sb(f"xn_q{i}", [P, QT, C]) for i in range(2)]
        xr_q = [sb(f"xr_q{i}", [P, QT, C]) for i in range(2)]
        w1_in = [sb(f"w1_in{i}", [P, HID]) for i in range(2)]
        w2_in = [sb(f"w2_in{i}", [P, HID]) for i in range(2)]
        gains = sb("gains", [P, E])
        cent = sb("cent", [P, ER])
        rank = sb("rank", [P, TILES, ER])
        st = sb("st", [P, QT, 6])
        mv = sb("mv", [P, QT, 2])
        var_eps = sb("var_eps", [P, QT])
        sd = sb("sd", [P, QT])
        rstd = sb("rstd", [P, QT])
        squares = sb("squares", [P, QT, C])
        ssum = sb("ssum", [P, QT])
        ms_eps = sb("ms_eps", [P, QT])
        rms = sb("rms", [P, QT])
        rrms = sb("rrms", [P, QT])
        th = sb("th", [P, TILES, ER])
        score = sb("score", [P, TILES, ER])
        left = sb("left", [P, TILES, ER])
        hit = sb("hit", [P, TILES, ER])
        pick = [sb(f"pick{i}", [P, TILES, ER]) for i in range(2)]
        best = sb("best", [P, TILES])
        total = sb("total", [P, TILES])
        rtotal = sb("rtotal", [P, TILES])
        gate = sb("gate", [P, TILES, ER])
        gateT = sb("gateT", [P, 2, P])

        tr_n = [psum[0], psum[1]]
        tr_r = [psum[2], psum[3]]
        logit = psum[4]
        tr_g = psum[5]

        const_in = sem("p_const_in")
        passed = sem("p_passed")
        x_in = [sem(f"p_x_in{i}") for i in range(2)]
        w1_ld = [sem(f"p_w1_in{i}") for i in range(2)]
        w2_ld = [sem(f"p_w2_in{i}") for i in range(2)]
        w1_used = sem("p_w1_used")
        w2_used = sem("p_w2_used")
        w2_hi = sem("p_w2_hi")
        w1_hi = sem("p_w1_hi")
        own = sem("p_own")
        route = sem("p_route")
        var_ok = sem("p_var_ok")
        sd_ok = sem("p_sd_ok")
        xn_ok = sem("p_xn_ok")
        ss_ok = sem("p_ss_ok")
        ms_ok = sem("p_ms_ok")
        rms_ok = sem("p_rms_ok")
        xr_ok = sem("p_xr_ok")
        xr_hi = sem("p_xr_hi")
        xnT_full = sem("p_xnT_full")
        xnT_out = sem("p_xnT_out")
        xrT_full = sem("p_xrT_full")
        xrT_out = sem("p_xrT_out")
        logit_ok = sem("p_logit_ok")
        th_ok = sem("p_th_ok")
        gate_ok = sem("p_gate_ok")
        gateT_full = sem("p_gateT_full")
        gateT_ok = sem("p_gateT_ok")
        gateT_st = sem("p_gateT_st")

        ident = keep["ident"]
        xnT = keep["xnT"]
        block = ctx.enter_context(nc.Block())

        @block.sync
        def _(sp):
            x_v = io["x"].rearrange("b (t p) c -> b p t c", p=P)
            for i in range(2):
                sp.dma_start(x_q[i][:, :, :], x_v[i, :, :, :]).then_inc(x_in[i], 16)
                if i == 0:
                    sp.dma_start(ident[:, :], io["ident"]).then_inc(const_in, 16)
                    sp.dma_start(gains[:, :], io["gains"]).then_inc(const_in, 16)
                    sp.dma_start(cent[:, :], io["cent"]).then_inc(const_in, 16)
                    sp.dma_start(rank[:, :, :], io["rank"]).then_inc(const_in, 16)
            sp.dma_start(w1_in[0][:, :], io["w1"][:, 0, :]).then_inc(w1_ld[0], 16)
            sp.dma_start(w1_in[1][:, :], io["w1"][:, 1, :]).then_inc(w1_ld[1], 16)
            for i in range(2):
                sp.wait_ge(xn_ok, QT * (i + 1))
                sp.dma_start(x_q[i][:, :, :], x_v[2 + i, :, :, :]).then_inc(x_in[i], 16)
            with sp.Fori(1, E // 2) as pair:
                for i in range(2):
                    wait_apart(sp, w1_used, pair * 2 + i - 1, passed)
                    sp.dma_start(w1_in[i][:, :], io["w1"][:, bass.ds(pair * 2 + i, 1), :]
                                 .rearrange("p a n -> p (a n)")).then_inc(w1_ld[i], 16)
            sp.wait_ge(gateT_ok, 1)
            for h in range(2):
                sp.dma_start(io["gate_scratch"][h * P:(h + 1) * P, :], gateT[:, h, :]).then_inc(gateT_st, 16)
            sp.wait_ge(gateT_st, 32)

        @block.gpsimd
        def _(pool):
            for i in range(2):
                pool.dma_start(w2_in[i][:, :], io["w2"][:, i, :]).then_inc(w2_ld[i], 16)

            def split_pair(pair, more):
                for i in range(2):
                    e = pair * 2 + i
                    hi = ffn["w2h"][:, bass.ds(e, 1), :].rearrange("p a n -> p (a n)")
                    lo = ffn["w2l"][:, bass.ds(e, 1), :].rearrange("p a n -> p (a n)")
                    wait_apart(pool, w2_ld[i], 16 * (pair + 1), passed)
                    nc.gpsimd.tensor_copy(hi, w2_in[i][:, :]).then_inc(w2_hi, 1)
                    pool.wait_ge(w2_hi, e + 1)
                    nc.gpsimd.tensor_tensor(lo, w2_in[i][:, :], hi.bitcast(F32), ALU.subtract).then_inc(w2_used, 1)
                    if more:
                        wait_apart(pool, w2_used, e + 1, passed)
                        pool.dma_start(w2_in[i][:, :], io["w2"][:, bass.ds(e + 2, 1), :]
                                       .rearrange("p a n -> p (a n)")).then_inc(w2_ld[i], 16)

            with pool.Fori(0, E // 2 - 1) as pair:
                split_pair(pair, True)
            split_pair(E // 2 - 1, False)

        @block.vector
        def _(dve):
            with dve.Fori(0, B // 2) as pair:
                for i in range(2):
                    b = pair * 2 + i
                    own_steps = Chain(dve, own, b * STEPS, passed)
                    dve.wait_ge(x_in[i], 16 * (pair + 1))
                    for t in range(QT):
                        last = nc.vector.bn_stats(st[:, t, :], x_q[i][:, t, :])
                    own_steps.did(last)
                    own_steps.settle(apart=True)
                    for t in range(QT):
                        last = nc.vector.bn_aggr(mv[:, t, :], st[:, t, :])
                    own_steps.did(last)
                    own_steps.settle()
                    nc.vector.tensor_scalar(var_eps[:, :], mv[:, :, 1], LN_EPS, None, ALU.add).then_inc(var_ok, 1)
                    dve.wait_ge(sd_ok, b + 1)
                    own_steps.did(nc.vector.reciprocal(rstd[:, :], sd[:, :]))
                    own_steps.settle()
                    dve.wait_ge(xnT_full, 2 * b + 2)
                    for t in range(QT):
                        nc.vector.tensor_scalar(xn_q[i][:, t, :], x_q[i][:, t, :], mv[:, t, 0:1], rstd[:, t:t + 1],
                                                ALU.subtract, ALU.mult).then_inc(xn_ok, 1)
                    dve.wait_ge(ss_ok, QT * (b + 1))
                    nc.vector.tensor_scalar(ms_eps[:, :], ssum[:, :], 1.0 / C, RMS_EPS,
                                            ALU.mult, ALU.add).then_inc(ms_ok, 1)
                    dve.wait_ge(rms_ok, b + 1)
                    own_steps.did(nc.vector.reciprocal(rrms[:, :], rms[:, :]))
                    own_steps.settle()
                    dve.wait_ge(xn_ok, QT * (b + 1))
                    for t in range(QT):
                        nc.vector.tensor_scalar(xr_q[i][:, t, :], xn_q[i][:, t, :], rrms[:, t:t + 1], None,
                                                ALU.mult).then_inc(xr_ok, 1)
                    for h in range(2):
                        cols = bass.ds(b * T + h * CH, CH)
                        dve.wait_ge(xrT_full, 2 * b + h + 1)
                        nc.vector.tensor_copy(ffn["xrh"][:, cols], tr_r[h][:, :]).then_inc(xr_hi, 1)
                        dve.wait_ge(xr_hi, 2 * b + h + 1)
                        nc.vector.tensor_tensor(ffn["xrl"][:, cols], tr_r[h][:, :],
                                                ffn["xrh"][:, cols].bitcast(F32), ALU.subtract).then_inc(xrT_out, 1)
                    assert own_steps.n == STEPS

            dve.wait_ge(const_in, 64)
            with dve.Fori(0, E // 2) as pair:
                for i in range(2):
                    e = pair * 2 + i
                    hi = ffn["w1h"][:, bass.ds(e, 1), :].rearrange("p a n -> p (a n)")
                    lo = ffn["w1l"][:, bass.ds(e, 1), :].rearrange("p a n -> p (a n)")
                    dve.wait_ge(w1_ld[i], 16 * (pair + 1))
                    gain = gains[:, bass.ds(e, 1)]
                    nc.vector.tensor_scalar(hi, w1_in[i][:, :], gain, None, ALU.mult).then_inc(w1_hi, 1)
                    dve.wait_ge(w1_hi, e + 1)
                    nc.vector.scalar_tensor_tensor(lo, w1_in[i][:, :], gain, hi.bitcast(F32),
                                                   ALU.mult, ALU.subtract).then_inc(w1_used, 1)

            def wide(m):
                return m.rearrange("p (t a) -> p t a", a=1).broadcast_to([P, TILES, ER])

            r = Chain(dve, route)
            dve.wait_ge(th_ok, 1)
            r.did(nc.vector.tensor_scalar(score[:, :, :], th[:, :, :], 0.5, 0.5, ALU.mult, ALU.add))
            r.settle()
            r.did(nc.vector.reduce_sum(total[:, :], score[:, :, :], axis=AX.X))
            r.settle()
            r.did(nc.vector.reciprocal(rtotal[:, :], total[:, :]))
            for k in range(2):
                src = score if k == 0 else left
                r.did(nc.vector.reduce_max(best[:, :], src[:, :, :], axis=AX.X))
                r.settle()
                r.did(nc.vector.tensor_tensor(hit[:, :, :], src[:, :, :], wide(best[:, :]), ALU.is_ge))
                r.settle()
                r.did(nc.vector.tensor_tensor(hit[:, :, :], hit[:, :, :], rank[:, :, :], ALU.mult))
                r.settle()
                r.did(nc.vector.reduce_max(best[:, :], hit[:, :, :], axis=AX.X))
                r.settle()
                r.did(nc.vector.tensor_tensor(pick[k][:, :, :], hit[:, :, :], wide(best[:, :]), ALU.is_equal))
                r.settle()
                if k == 0:
                    r.did(nc.vector.scalar_tensor_tensor(left[:, :, :], pick[0][:, :, :], -4.0, score[:, :, :],
                                                         ALU.mult, ALU.add))
                    r.settle()
            r.did(nc.vector.tensor_tensor(pick[0][:, :, :], pick[0][:, :, :], pick[1][:, :, :], ALU.add))
            r.settle()
            r.did(nc.vector.tensor_tensor(gate[:, :, :], pick[0][:, :, :], score[:, :, :], ALU.mult))
            r.settle()
            nc.vector.tensor_tensor(gate[:, :, :], gate[:, :, :], wide(rtotal[:, :]), ALU.mult).then_inc(gate_ok, 1)
            dve.wait_ge(gateT_full, 2)
            nc.vector.tensor_copy(gateT[:, :, :].rearrange("p h n -> p (h n)"), tr_g[:, 0:2 * P]).then_inc(gateT_ok, 1)

        @block.scalar
        def _(act):
            with act.Fori(0, B // 2) as pair:
                for i in range(2):
                    b = pair * 2 + i
                    act.wait_ge(var_ok, b + 1)
                    nc.scalar.activation(sd[:, :], var_eps[:, :], ACT.Sqrt).then_inc(sd_ok, 1)
                    for t in range(QT):
                        act.wait_ge(xn_ok, QT * b + t + 1)
                        nc.scalar.activation(squares[:, t, :], xn_q[i][:, t, :], ACT.Square,
                                             accum_out=ssum[:, t:t + 1]).then_inc(ss_ok, 1)
                    act.wait_ge(ms_ok, b + 1)
                    nc.scalar.activation(rms[:, :], ms_eps[:, :], ACT.Sqrt).then_inc(rms_ok, 1)
                    for h in range(2):
                        act.wait_ge(xnT_full, 2 * b + h + 1 + 4)
                        nc.scalar.activation(xnT[:, bass.ds(b * T + h * CH, CH)], tr_n[h][:, :],
                                             ACT.Copy).then_inc(xnT_out, 1)
            act.wait_ge(logit_ok, 1)
            nc.scalar.activation(th[:, :, :], logit[:, 0:TILES * ER].rearrange("p (t e) -> p t e", e=ER),
                                 ACT.Tanh, scale=0.5).then_inc(th_ok, 1)

        @block.tensor
        def _(pe):
            pe.wait_ge(const_in, 64)
            pe.sem_inc(xnT_full, 4)
            with pe.Fori(0, B // 2) as pair:
                for i in range(2):
                    b = pair * 2 + i
                    for h in range(2):
                        pe.wait_ge(xn_ok, QT * b + 4 * (h + 1))
                        pe.wait_ge(xnT_out, 2 * b)
                        for k in range(4):
                            last = nc.tensor.transpose(tr_n[h][:, k * P:(k + 1) * P], xn_q[i][:, 4 * h + k, :],
                                                       ident[:, :])
                        last.then_inc(xnT_full, 1)
                    for h in range(2):
                        pe.wait_ge(xr_ok, QT * b + 4 * (h + 1))
                        pe.wait_ge(xrT_out, 2 * b)
                        for k in range(4):
                            last = nc.tensor.transpose(tr_r[h][:, k * P:(k + 1) * P], xr_q[i][:, 4 * h + k, :],
                                                       ident[:, :])
                        last.then_inc(xrT_full, 1)
            pe.wait_ge(xnT_out, 2 * B)
            for t in range(TILES):
                last = nc.tensor.matmul(logit[:, t * ER:(t + 1) * ER], xnT[:, t * P:(t + 1) * P], cent[:, :],
                                        start=True, stop=True)
            last.then_inc(logit_ok, 1)
            pe.wait_ge(gate_ok, 1)
            flat = gate[:, :, :].rearrange("p t e -> p (t e)")
            for h in range(2):
                nc.tensor.transpose(tr_g[:, h * P:(h + 1) * P], flat[:, h * P:(h + 1) * P],
                                    ident[:, :]).then_inc(gateT_full, 1)


def experts(nc, keep, ffn, io, psum):
    NQ = E * HT
    NY = 1 + ER
    LAG = 3
    HB = 4
    TAIL_AT, CONV_AT = 10, 22
    with ExitStack() as ctx:
        def sb(name, shape, dt=F32):
            return ctx.enter_context(nc.sbuf_tensor(name, shape, dt))

        def sem(name):
            return ctx.enter_context(nc.semaphore(name))

        hidden = [sb(f"hidden{i}", [P, CH]) for i in range(2)]
        hid_hi = [sb(f"hid_hi{i}", [P, CH], F32R) for i in range(HB)]
        hid_lo = [sb(f"hid_lo{i}", [P, CH], F32R) for i in range(HB)]
        gates = [sb(f"gates{i}", [P, CH]) for i in range(2)]
        gated = [sb(f"gated{i}", [P, CH]) for i in range(2)]
        acc = [sb(f"acc{i}", [P, CH]) for i in range(2)]
        tanh_g = sb("tanh_g", [P, CH])
        silu_g = sb("silu_g", [P, CH])
        lepe_g = sb("lepe_g", [P, CH])
        x_c = sb("x_c", [P, CT, C])
        rest = sb("rest", [P, CT, C])
        v_pad = sb("v_pad", [P, T + 2])
        lepe = sb("lepe", [P, T])
        b1 = sb("b1", [P, E * HT])
        b2 = sb("b2", [P, E])
        b2s = sb("b2s", [P, 1])
        wv = sb("wv", [P, C])
        cols = sb("cols", [P, 5])

        hid_ps = psum[0:HB]
        y_ps = psum[4:6]
        aux = [psum[6], psum[7]]

        const_in = sem("f_const_in")
        passed = sem("f_passed")
        ready = sem("f_ready")
        hid_full = sem("f_hid_full")
        gelu_ok = sem("f_gelu_ok")
        hi_ok = sem("f_hi_ok")
        split_ok = sem("f_split_ok")
        down_ok = sem("f_down_ok")
        y_out = sem("f_y_out")
        gates_in = [sem(f"f_gates_in{i}") for i in range(2)]
        acc_ok = sem("f_acc_ok")
        tanh_ok = sem("f_tanh_ok")
        pool_own = sem("f_pool_own")
        tail_ok = sem("f_tail_ok")
        aux_full = sem("f_aux_full")
        silu_out = sem("f_silu_out")
        rest_ok = sem("f_rest_ok")
        x_c_in = sem("f_x_c_in")
        rest_st = sem("f_rest_st")
        v_full = sem("f_v_full")
        v_ok = sem("f_v_ok")
        conv_own = sem("f_conv_own")
        conv_ok = sem("f_conv_ok")

        ident, xnT, silu_t = keep["ident"], keep["xnT"], keep["silu_t"]
        block = ctx.enter_context(nc.Block())

        def chunks(eng, body):
            body(0, 0, False)
            with eng.Fori(0, (NCH - 2) // 2) as pair:
                body(pair * 2 + 1, 1, True)
                body(pair * 2 + 2, 0, True)
            body(NCH - 1, 1, True)

        def gate_slot(y):
            return (y - 1) % 2

        @block.sync
        def _(sp):
            for dst, src in ((b1, "b1"), (b2, "b2"), (wv, "wv"), (cols, "cols")):
                sp.dma_start(dst[:, :], io[src]).then_inc(const_in, 16)
            gate_v = io["gate_scratch"].rearrange("(c t e) n -> c e t n", t=CT, e=ER)
            x_v = io["x"].rearrange("b (h t p) c -> (b h) p t c", p=P, t=CT)
            rest_v = io["rest_scratch"].rearrange("(c t p) n -> c p t n", p=P, t=CT)

            def load_x(c):
                sp.dma_start(x_c[:, :, :], x_v[bass.ds(c, 1), :, :, :].rearrange("a p t c -> p (a t) c"))\
                  .then_inc(x_c_in, 16)

            def store_rest(c):
                wait_apart(sp, rest_ok, c + 1, passed)
                sp.dma_start(rest_v[bass.ds(c, 1), :, :, :].rearrange("a p t c -> p (a t) c"), rest[:, :, :])\
                  .then_inc(rest_st, 16)

            def body(c, par, tail):
                for y in range(1, NY):
                    wait_apart(sp, y_out, c * NY + (y if y <= 2 else y + 1), passed)
                    src = gate_v[bass.ds(c, 1), y - 1, :, :]
                    sp.dma_start(gates[gate_slot(y)][:, :].rearrange("p (t n) -> p t n", n=P),
                                 src.broadcast_to([P, CT, P])).then_inc(gates_in[gate_slot(y)], 16)
                    if y == 4 and tail:
                        store_rest(c - 1)
                        load_x(c)

            load_x(0)
            chunks(sp, body)
            store_rest(NCH - 1)
            sp.wait_ge(rest_st, 16 * NCH)

        @block.tensor
        def _(pe):
            pe.sem_inc(down_ok, HB)
            pe.wait_ge(const_in, 64)

            def up(c, q):
                e, ht = q // HT, q % HT
                toks = bass.ds(c * CH, CH)
                m = slice(ht * P, (ht + 1) * P)
                bank = hid_ps[q % HB]
                pe.wait_ge(gelu_ok, c * NQ + q + 1)
                nc.tensor.matmul(bank[:, :], ffn["w1h"][:, e, m], ffn["xrh"][:, toks], start=True, stop=False)
                nc.tensor.matmul(bank[:, :], ffn["w1h"][:, e, m], ffn["xrl"][:, toks], start=False, stop=False)
                nc.tensor.matmul(bank[:, :], ffn["w1l"][:, e, m], ffn["xrh"][:, toks], start=False, stop=True)\
                  .then_inc(hid_full, 1)

            def down(c, par, q):
                e, ht = q // HT, q % HT
                y = max(0, e - ES + 1)
                first, last = q in (0, *range(ES * HT, NQ, HT)), ht == HT - 1 and e >= ES - 1
                bank = y_ps[(par + y) % 2]
                m = slice(ht * P, (ht + 1) * P)
                if first:
                    pe.wait_ge(y_out, c * NY + y + 1)
                pe.wait_ge(split_ok, c * NQ + q + 1 + 2)
                nc.tensor.matmul(bank[:, :], ffn["w2h"][:, e, m], hid_hi[q % HB][:, :], start=first, stop=False)
                nc.tensor.matmul(bank[:, :], ffn["w2l"][:, e, m], hid_hi[q % HB][:, :], start=False, stop=False)
                nc.tensor.matmul(bank[:, :], ffn["w2h"][:, e, m], hid_lo[q % HB][:, :], start=False, stop=last)\
                  .then_inc(down_ok, 1)

            def tail_transposes(c):
                pe.wait_ge(tail_ok, c + 1)
                pe.wait_ge(v_ok, 2 * (c // 2) + 2)
                for bank, src in ((aux[0], silu_g), (aux[1], lepe_g)):
                    for t in range(CT):
                        last = nc.tensor.transpose(bank[:, t * P:(t + 1) * P], src[:, t * P:(t + 1) * P], ident[:, :])
                    last.then_inc(aux_full, 1)

            def v_product(b, after):
                pe.wait_ge(silu_out, after)
                pe.wait_ge(rest_ok, after)
                for h in range(2):
                    nc.tensor.matmul(aux[h][:, :], wv[:, :], xnT[:, bass.ds(b * T + h * CH, CH)],
                                     start=True, stop=True).then_inc(v_full, 1)

            def body(c, par, tail):
                for q in range(NQ + LAG):
                    if q < NQ:
                        up(c, q)
                    if q == TAIL_AT and tail:
                        tail_transposes(c - 1)
                    if q == CONV_AT and par == 0:
                        v_product(c // 2, c)
                    if q >= LAG:
                        down(c, par, q - LAG)

            chunks(pe, body)
            tail_transposes(NCH - 1)

        @block.scalar
        def _(act):
            act.sem_inc(gelu_ok, HB)
            act.wait_ge(const_in, 64)

            def tanh_part(c, par):
                act.wait_ge(acc_ok, (c + 1) * ER)
                nc.scalar.activation(tanh_g[:, :], acc[par][:, :], ACT.Tanh, scale=0.5).then_inc(tanh_ok, 1)

            def silu_part(c):
                act.wait_ge(aux_full, 2 * c + 1)
                nc.scalar.activation(silu_t[:, bass.ds(c * CT, CT), :],
                                     aux[0][:, :].rearrange("p (t n) -> p t n", n=P), ACT.Copy).then_inc(silu_out, 1)

            def body(c, par, tail):
                for q in range(NQ):
                    act.wait_ge(hid_full, c * NQ + q + 1)
                    act.wait_ge(split_ok, c * NQ + q + 1)
                    nc.scalar.activation(hidden[q % 2][:, :], hid_ps[q % HB][:, :], ACT.Gelu,
                                         bias=b1[:, q:q + 1]).then_inc(gelu_ok, 1)
                    if q == 3 and tail:
                        tanh_part(c - 1, 1 - par)
                    if q == TAIL_AT + 1 and tail:
                        silu_part(c - 1)
                    if q == CONV_AT + 1 and par == 0:
                        for h in range(2):
                            act.wait_ge(v_full, c + h + 1)
                            act.wait_ge(conv_ok, c // 2)
                            nc.scalar.activation(v_pad[:, 1 + h * CH:1 + (h + 1) * CH], aux[h][:, :],
                                                 ACT.Identity, bias=cols[:, 4:5]).then_inc(v_ok, 1)

            chunks(act, body)
            tanh_part(NCH - 1, 1)
            silu_part(NCH - 1)

        @block.vector
        def _(dve):
            dve.sem_inc(split_ok, 2)
            dve.sem_inc(y_out, 2)
            nc.vector.memset(v_pad[:, 0:1], 0.0)
            nc.vector.memset(v_pad[:, T + 1:T + 2], 0.0).then_inc(ready, 1)
            dve.wait_ge(const_in, 64)
            nc.vector.tensor_tensor(b2s[:, :], b2[:, 0:1], b2[:, 1:2], ALU.add).then_inc(ready, 1)
            dve.wait_ge(ready, 2)

            def split(c, q):
                dve.wait_ge(gelu_ok, c * NQ + q + 1 + HB)
                dve.wait_ge(down_ok, c * NQ + q + 1)
                nc.vector.tensor_copy(hid_hi[q % HB][:, :], hidden[q % 2][:, :]).then_inc(hi_ok, 1)
                dve.wait_ge(hi_ok, c * NQ + q + 1)
                nc.vector.tensor_tensor(hid_lo[q % HB][:, :], hidden[q % 2][:, :], hid_hi[q % HB][:, :].bitcast(F32),
                                        ALU.subtract).then_inc(split_ok, 1)

            def output(c, par, y):
                dve.wait_ge(down_ok, c * NQ + (ES + y) * HT + HB)
                bank = y_ps[(par + y) % 2]
                if y == 0:
                    nc.vector.scalar_tensor_tensor(acc[par][:, :], bank[:, :], b2s[:, 0:1],
                                                   xnT[:, bass.ds(c * CH, CH)], ALU.add, ALU.add)\
                      .then_inc(y_out, 1)
                    return
                slot = gate_slot(y)
                dve.wait_ge(gates_in[slot], 16 * (ER // 2) * c + 16 * ((y - 1) // 2 + 1))
                if y > 2 or not (type(c) is int and c == 0):
                    dve.wait_ge(acc_ok, c * ER + y - 2)
                nc.vector.scalar_tensor_tensor(gated[slot][:, :], bank[:, :], b2[:, ES + y - 1:ES + y],
                                               gates[slot][:, :], ALU.add, ALU.mult).then_inc(y_out, 1)

            def rest_part(c):
                dve.wait_ge(aux_full, 2 * c + 2)
                dve.wait_ge(x_c_in, 16 * (c + 1))
                dve.wait_ge(rest_st, 16 * c)
                nc.vector.tensor_tensor(rest[:, :, :], aux[1][:, :].rearrange("p (t n) -> p t n", n=P),
                                        x_c[:, :, :], ALU.add).then_inc(rest_ok, 1)

            def convolve(b, tails):
                dve.wait_ge(v_ok, 2 * b + 2)
                dve.wait_ge(tail_ok, tails)
                nc.vector.tensor_scalar(lepe[:, :], v_pad[:, 1:T + 1], cols[:, 1:2], cols[:, 3:4],
                                        ALU.mult, ALU.add).then_inc(conv_own, 1)
                dve.wait_ge(conv_own, 2 * b + 1)
                nc.vector.scalar_tensor_tensor(lepe[:, :], v_pad[:, 0:T], cols[:, 0:1], lepe[:, :],
                                               ALU.mult, ALU.add).then_inc(conv_own, 1)
                dve.wait_ge(conv_own, 2 * b + 2)
                nc.vector.scalar_tensor_tensor(lepe[:, :], v_pad[:, 2:T + 2], cols[:, 2:3], lepe[:, :],
                                               ALU.mult, ALU.add).then_inc(conv_ok, 1)

            def body(c, par, tail):
                for q in range(NQ):
                    split(c, q)
                    if q == TAIL_AT + 2 and tail:
                        rest_part(c - 1)
                    if q == CONV_AT + 3 and par == 0:
                        convolve(c // 2, c)
                    e, ht = (q - LAG - 1) // HT, (q - LAG - 1) % HT
                    if q > LAG and ht == HT - 1 and e >= ES - 1:
                        output(c, par, e - ES + 1)
                output(c, par, NY - 1)

            chunks(dve, body)
            rest_part(NCH - 1)

        @block.gpsimd
        def _(pool):
            def add(c, par, y):
                pool.wait_ge(y_out, c * NY + y + 1 + 2)
                pool.wait_ge(acc_ok, c * ER + y - 1)
                nc.gpsimd.tensor_tensor(acc[par][:, :], acc[par][:, :], gated[gate_slot(y)][:, :],
                                        ALU.add).then_inc(acc_ok, 1)

            def tail_part(c, par):
                wait_apart(pool, tanh_ok, c + 1, passed)
                own = Chain(pool, pool_own, 2 * c)
                own.did(nc.gpsimd.tensor_scalar(tanh_g[:, :], tanh_g[:, :], 0.5, 0.5, ALU.mult, ALU.add))
                own.settle()
                if not (type(c) is int and c == 0):
                    pool.wait_ge(aux_full, 2 * c)
                own.did(nc.gpsimd.tensor_tensor(silu_g[:, :], acc[par][:, :], tanh_g[:, :], ALU.mult))
                own.settle()
                pool.wait_ge(conv_ok, c // 2 + 1)
                nc.gpsimd.tensor_tensor(lepe_g[:, :], lepe[:, par * CH:(par + 1) * CH], silu_g[:, :],
                                        ALU.mult).then_inc(tail_ok, 1)

            def body(c, par, tail):
                if tail:
                    tail_part(c - 1, 1 - par)
                for y in range(1, NY):
                    add(c, par, y)

            chunks(pool, body)
            tail_part(NCH - 1, 1)


def attention(nc, keep, io, psum):
    N = B * HG
    KT = T // P
    QH = T // CH
    SLOTS = QH * KT * J
    GROUPS = QH * KT
    PAIRS = KT * J
    W = 3 * GF
    ROWS = 32
    HI0, SECOND, THIRD, SHIFT = 0, D, 2 * D, 3 * D
    FRONT_ROUNDS, ROUNDS = 6, 10
    POOL_FRONT, POOL_MAX, POOL_OUT = 12, 2, 1
    POOL_STEPS = POOL_FRONT + QH * POOL_MAX + QH * POOL_OUT
    AT_SHIFT1, AT_QKV, AT_K, AT_Q, AT_SHIFT0 = 12, (2, 5), (44, 47), (50, 53), 40

    with ExitStack() as ctx:
        def sb(name, shape, dt=F32):
            return ctx.enter_context(nc.sbuf_tensor(name, shape, dt))

        def sem(name):
            return ctx.enter_context(nc.semaphore(name))

        x_cur = [sb(f"x_cur{i}", [P, T]) for i in range(2)]
        w_cur = [sb(f"w_cur{i}", [P, W]) for i in range(2)]
        w_all = sb("w_all", [P, HG, W])
        bias = sb("bias", [P, HG, W])
        cosine = sb("cosine", [P, KT, D // 2])
        sine = sb("sine", [P, KT, D // 2])
        pre = sb("pre", [P, KT, W])
        expd = sb("expd", [P, KT, 2 * GF])
        feat = sb("feat", [P, KT, 2 * J, D])
        rope = [sb(f"rope{i}", [P, KT, 2 * J, D // 2]) for i in range(4)]
        turned = sb("turned", [P, KT, 2 * J, D])
        stage = [sb(f"stage{i}", [P, KT, 2 * J, ROWS], F32R) for i in range(2)]
        v_raw = [sb(f"v_raw{i}", [P, KT, J, D]) for i in range(2)]
        v_st = [sb(f"v_st{i}", [P, KT, J, ROWS]) for i in range(2)]
        k_raw = [sb(f"k_raw{i}", [P, T], F32R) for i in range(2)]
        q_raw = [sb(f"q_raw{i}", [P, T], F32R) for i in range(2)]
        k_mask = [sb(f"k_mask{i}", [P, J, T], F32R) for i in range(2)]
        q_mask = [sb(f"q_mask{i}", [P, J, T], F32R) for i in range(2)]
        q_sh = [sb(f"q_sh{i}", [P, T], F32R) for i in range(2)]
        neg_max = [sb(f"neg_max{i}", [P, KT, J, 1]) for i in range(2)]
        prob = [sb(f"prob{i}", [P, J, CH]) for i in range(2)]
        pv_sb = sb("pv_sb", [P, CH])
        r_sum = sb("r_sum", [P, CT, J, 1])
        attn = [sb(f"attn{i}", [P, CT, J, D]) for i in range(2)]
        rest = [sb(f"rest_a{i}", [P, KT, GF]) for i in range(2)]
        result = [sb(f"result{i}", [P, CT, GF]) for i in range(2)]

        s_ps = [psum[0], psum[1]]
        m_ps = [psum["m0"], psum["m1"]]
        pv_ps = psum[6]
        bank = psum[7]

        const_in = sem("a_const_in")
        passed = sem("a_passed")
        ready = sem("a_ready")
        cur_ok = sem("a_cur_ok")
        round_full = sem("a_round_full")
        round_free = sem("a_round_free")
        pre_ok = sem("a_pre_ok")
        exp_f_ok = sem("a_exp_f_ok")
        pool_own = sem("a_pool_own")
        front_ok = sem("a_front_ok")
        raw_ok = sem("a_raw_ok")
        qmask_in = [sem(f"a_qmask_in{i}") for i in range(2)]
        kmask_in = [sem(f"a_kmask_in{i}") for i in range(2)]
        max_full = sem("a_max_full")
        max_ok = sem("a_max_ok")
        shift_ok = sem("a_shift_ok")
        q_sh_ok = sem("a_q_sh_ok")
        v_st_ok = sem("a_v_st_ok")
        s_full = sem("a_s_full")
        exp_ok = sem("a_exp_ok")
        pv_ok = sem("a_pv_ok")
        pv_out = sem("a_pv_out")
        rsum_ok = sem("a_rsum_ok")
        attn_ok = sem("a_attn_ok")
        res_ok = sem("a_res_ok")
        rest_in = [sem(f"a_rest_in{i}") for i in range(2)]
        res_st = [sem(f"a_res_st{i}") for i in range(2)]

        ident, xnT, silu_t = keep["ident"], keep["xnT"], keep["silu_t"]
        block = ctx.enter_context(nc.Block())

        def items(eng, body):
            for n in (-2, -1, 0):
                body(n, n % 2)
            with eng.Fori(0, (N - 4) // 2) as pair:
                body(pair * 2 + 1, 1)
                body(pair * 2 + 2, 0)
            for n in range(N - 3, N):
                body(n, n % 2)

        def has(n):
            if type(n) is not int:
                return True, True, True
            return n >= 0, 0 <= n + 1 < N, n + 2 < N

        def rounds_before(n):
            if type(n) is not int or 0 <= n <= N - 2:
                return 2 * FRONT_ROUNDS + 1 + ROUNDS * n
            if n < 0:
                return FRONT_ROUNDS * (n + 2)
            return rounds_before(N - 2) + ROUNDS - FRONT_ROUNDS

        def schedule(n):
            a, m, f = has(n)
            out = []
            if f:
                out += [(AT_QKV[h], "qkv", h) for h in range(2)]
            if a:
                out += [(AT_SHIFT1, "shift", 1)]
            if a:
                out += [(SLOTS // 2 + 5, "out", 0)]
            if m:
                out += [(AT_SHIFT0, "shift", 0)]
            if f:
                out += [(AT_K[h], "k", h) for h in range(2)] + [(AT_Q[h], "q", h) for h in range(2)]
            if a:
                out += [(SLOTS, "out", 1)]
            return [(*r, i) for i, r in enumerate(sorted(out, key=lambda r: r[0]))]

        def at(n, slot):
            return [(kind, part, rounds_before(n) + i) for s, kind, part, i in schedule(n) if s == slot]

        @block.sync
        def _(sp):
            for dst, src in ((w_all, "wqkv"), (bias, "bqkv"), (cosine, "cosine"), (sine, "sine")):
                sp.dma_start(dst[:, :, :], io[src]).then_inc(const_in, 16)
            rest_v = io["rest_scratch"].rearrange("(b t p) (g f) -> p b g t f", p=P, t=KT, f=GF)
            out_v = io["out"].rearrange("b (h t p) (g f) -> p b g h t f", p=P, t=CT, f=GF)

            def body(n, par):
                a, m, f = has(n)
                if a:
                    if not (type(n) is int and n < 2):
                        wait_apart(sp, res_ok, 2 * (n - 1), passed)
                    src = rest_v[:, bass.ds(n // HG, 1), bass.ds(n % HG, 1), :, :]
                    sp.dma_start(rest[par][:, :, :], src.rearrange("p b g t f -> p (b g t) f"))\
                      .then_inc(rest_in[par], 16)
                if m:
                    wait_apart(sp, raw_ok, 4 * (n + 2), passed)
                    if a:
                        sp.wait_ge(s_full, SLOTS * n)
                    for j in range(J):
                        sp.dma_start(k_mask[1 - par][j * ROWS:(j + 1) * ROWS, j, :].bitcast(F32),
                                     k_raw[1 - par][j * ROWS:(j + 1) * ROWS, :].bitcast(F32)).then_inc(kmask_in[1 - par], 16)
                if a:
                    store(n, 0)
                if f:
                    wait_apart(sp, raw_ok, 4 * (n + 3), passed)
                    if a:
                        sp.wait_ge(max_full, PAIRS * (n + 1))
                    for j in range(J):
                        rows = slice(j * ROWS, j * ROWS + SHIFT)
                        sp.dma_start(q_mask[par][rows, j, :].bitcast(F32),
                                     q_raw[par][rows, :].bitcast(F32)).then_inc(qmask_in[par], 16)
                if a:
                    store(n, 1)

            def store(n, h):
                wait_apart(sp, res_ok, 2 * n + h + 1, passed)
                dst = out_v[:, bass.ds(n // HG, 1), bass.ds(n % HG, 1), h, :, :]
                sp.dma_start(dst.rearrange("p b g t f -> p (b g t) f"), result[h][:, :, :]).then_inc(res_st[h], 16)

            sp.wait_ge(ready, 5)
            items(sp, body)
            for h in range(2):
                sp.wait_ge(res_st[h], 16 * N)

        @block.gpsimd
        def _(pool):
            for i in range(2):
                nc.gpsimd.memset(v_st[i][:, :, :, D:ROWS], 0.0)
            nc.gpsimd.memset(q_mask[1][:, :, :].bitcast(F32), 0.0).then_inc(ready, 1)
            pool.wait_ge(const_in, 64)

            def front(f, par, base):
                own = Chain(pool, pool_own, base, passed)
                if not (type(f) is int and f < 2):
                    wait_apart(pool, pre_ok, 2 * (f - 1), passed)
                nc.gpsimd.tensor_copy(x_cur[par][:, :], xnT[:, bass.ds((f // HG) * T, T)]).then_inc(cur_ok, 1)
                nc.gpsimd.tensor_copy(w_cur[par][:, :], w_all[:, bass.ds(f % HG, 1), :]
                                      .rearrange("p a n -> p (a n)")).then_inc(cur_ok, 1)
                pool.wait_ge(exp_f_ok, f + 1)
                wait_apart(pool, pre_ok, 2 * (f + 1), passed)
                qk = pre[:, :, 0:2 * GF]
                flat = feat[:, :, :, :].rearrange("p t j d -> p t (j d)")
                own.did(nc.gpsimd.tensor_scalar(flat, qk, 0.0, None, ALU.max))
                own.did(nc.gpsimd.tensor_scalar(expd[:, :, :], expd[:, :, :], 1.0, None, ALU.min))
                nc.gpsimd.tensor_copy(v_raw[par][:, :, :, :].rearrange("p t j d -> p t (j d)"),
                                      pre[:, :, 2 * GF:W]).then_inc(front_ok, 1)
                own.settle()
                own.did(nc.gpsimd.tensor_tensor(flat, flat, expd[:, :, :], ALU.add))
                own.settle()
                cos_w = cosine[:, :, :].rearrange("p t (a d) -> p t a d", a=1).broadcast_to([P, KT, 2 * J, D // 2])
                sin_w = sine[:, :, :].rearrange("p t (a d) -> p t a d", a=1).broadcast_to([P, KT, 2 * J, D // 2])
                even, odd = feat[:, :, :, 0:D:2], feat[:, :, :, 1:D:2]
                for dst, src, table in ((0, even, cos_w), (1, odd, sin_w), (2, even, sin_w), (3, odd, cos_w)):
                    own.did(nc.gpsimd.tensor_tensor(rope[dst][:, :, :, :], src, table, ALU.mult))
                own.settle()
                own.did(nc.gpsimd.tensor_tensor(turned[:, :, :, 0:D:2], rope[0][:, :, :, :], rope[1][:, :, :, :],
                                                ALU.subtract))
                own.did(nc.gpsimd.tensor_tensor(turned[:, :, :, 1:D:2], rope[2][:, :, :, :], rope[3][:, :, :, :],
                                                ALU.add))
                own.settle(apart=True)
                if not (type(f) is int and f < 2):
                    wait_apart(pool, q_sh_ok, 2 * (f - 1), passed)
                st = stage[par]
                own.did(nc.gpsimd.tensor_copy(st[:, :, :, HI0:D].rearrange("p t j d -> p (t j) d"),
                                              turned[:, :, :, :].rearrange("p t j d -> p (t j) d")))
                own.did(nc.gpsimd.tensor_copy(st[:, :, 0:J, THIRD:THIRD + D], turned[:, :, 0:J, :]))
                own.did(nc.gpsimd.tensor_copy(st[:, :, J:2 * J, SECOND:SECOND + D], turned[:, :, J:2 * J, :]))
                own.settle()
                nc.gpsimd.tensor_tensor(st[:, :, 0:J, SECOND:SECOND + D], turned[:, :, 0:J, :],
                                        st[:, :, 0:J, HI0:D].bitcast(F32), ALU.subtract).then_inc(front_ok, 1)
                nc.gpsimd.tensor_tensor(st[:, :, J:2 * J, THIRD:THIRD + D], turned[:, :, J:2 * J, :],
                                        st[:, :, J:2 * J, HI0:D].bitcast(F32), ALU.subtract).then_inc(front_ok, 1)
                assert own.n == POOL_FRONT

            def shift(m, par, h, base):
                own = Chain(pool, pool_own, base, passed)
                wait_apart(pool, max_ok, PAIRS * m + (h + 1) * PAIRS // 2 + 2, passed)
                ts = slice(h * CT, (h + 1) * CT)
                src = neg_max[par][:, ts, :, :]
                hi = stage[par][:, ts, 0:J, SHIFT:SHIFT + 1]
                own.did(nc.gpsimd.tensor_copy(hi, src))
                own.settle()
                own.did(nc.gpsimd.tensor_tensor(stage[par][:, ts, 0:J, SHIFT + 1:SHIFT + 2], src,
                                                hi.bitcast(F32), ALU.subtract))
                own.settle()
                pool.sem_inc(shift_ok, 1)
                assert own.n == POOL_MAX

            def values(m, par):
                if not (type(m) is int and m < 2):
                    pool.wait_ge(pv_ok, GROUPS * (m - 1) + 2)
                wait_apart(pool, front_ok, 3 * m + 1, passed)
                nc.gpsimd.tensor_copy(v_st[par][:, :, :, 0:D].rearrange("p t j d -> p (t j) d"),
                                      v_raw[par][:, :, :, :].rearrange("p t j d -> p (t j) d")).then_inc(v_st_ok, 1)

            def combine(n, par, h, base):
                own = Chain(pool, pool_own, base, passed)
                pool.wait_ge(attn_ok, 2 * n + h + 1)
                pool.wait_ge(rest_in[par], 16 * (n // 2 + 1))
                if not (type(n) is int and n == 0):
                    pool.wait_ge(res_st[h], 16 * n)
                a_v = attn[h][:, :, :, :].rearrange("p t j d -> p t (j d)")
                gate = silu_t[:, bass.ds((n // HG) * KT + h * CT, CT), bass.ds((n % HG) * GF, GF)]
                own.did(nc.gpsimd.tensor_tensor(result[h][:, :, :], a_v, gate, ALU.mult))
                own.settle()
                nc.gpsimd.tensor_tensor(result[h][:, :, :], result[h][:, :, :],
                                        rest[par][:, h * CT:(h + 1) * CT, :], ALU.add).then_inc(res_ok, 1)

            def body(n, par):
                a, m, f = has(n)
                if type(n) is not int or 0 <= n <= N - 2:
                    base = 2 * POOL_FRONT + POOL_MAX + POOL_STEPS * n
                elif n < 0:
                    base = POOL_FRONT * (n + 2)
                else:
                    base = 2 * POOL_FRONT + POOL_MAX + POOL_STEPS * (N - 2) + POOL_STEPS - POOL_FRONT
                if a:
                    shift(n, par, 1, base)
                    base = base + POOL_MAX
                if f:
                    front(n + 2, par, base)
                    base = base + POOL_FRONT
                if m:
                    values(n + 1, 1 - par)
                if a:
                    combine(n, par, 0, base)
                    base = base + POOL_OUT
                if m:
                    shift(n + 1, 1 - par, 0, base)
                    base = base + POOL_MAX
                if a:
                    combine(n, par, 1, base)

            items(pool, body)

        @block.tensor
        def _(pe):
            pe.wait_ge(ready, 5)
            pe.sem_inc(pv_ok, 2)

            def score(n, par, s):
                qh, kt, j = s // (KT * J), s // J % KT, s % J
                if s == 0:
                    pe.wait_ge(kmask_in[par], 16 * J * (n // 2 + 1))
                if s in (0, SLOTS // 2):
                    pe.wait_ge(q_sh_ok, 2 * n + qh + 1)
                pe.wait_ge(exp_ok, SLOTS * n + s + 1)
                nc.tensor.matmul(s_ps[s % 2][:, :], k_mask[par][:, j, kt * P:(kt + 1) * P],
                                 q_sh[par][:, qh * CH:(qh + 1) * CH], start=True, stop=True).then_inc(s_full, 1)

            def weigh(n, par, g):
                kt = g % KT
                if g == 0:
                    pe.wait_ge(v_st_ok, n + 1)
                if kt == 0:
                    pe.wait_ge(pv_out, QH * n + g // KT + 1)
                pe.wait_ge(exp_ok, SLOTS * n + J * (g + 1) + 2)
                for j in range(J):
                    last = nc.tensor.matmul(pv_ps[j * ROWS:(j + 1) * ROWS, :], v_st[par][:, kt, j, :],
                                            prob[g % 2][:, j, :], start=kt == 0, stop=kt == KT - 1)
                last.then_inc(pv_ok, 1)

            def maxima(m, par, k):
                qt, j = k // J, k % J
                if k == 0:
                    pe.wait_ge(qmask_in[par], 16 * J * (m // 2 + 1))
                    pe.wait_ge(raw_ok, 4 * (m + 1))
                pe.wait_ge(max_ok, PAIRS * m + k + 1)
                for kh in range(2):
                    last = nc.tensor.matmul(m_ps[k % 2][:, kh * CH:(kh + 1) * CH],
                                            q_mask[par][:, j, qt * P:(qt + 1) * P],
                                            k_raw[par][:, kh * CH:(kh + 1) * CH], start=True, stop=True)
                last.then_inc(max_full, 1)

            def rounds(n, par, slot):
                for kind, part, r in at(n, slot):
                    if kind == "qkv":
                        pe.wait_ge(cur_ok, 2 * (n + 3))
                    if kind in "kq":
                        pe.wait_ge(front_ok, 3 * (n + 3))
                    if kind == "shift":
                        pe.wait_ge(shift_ok, 2 * (n + (part == 0)) + part + 1)
                    if kind == "out":
                        pe.wait_ge(pv_out, QH * n + part + 1 + 1)
                    pe.wait_ge(round_free, r + 1)
                    for t in range(CT):
                        tile = part * CT + t
                        if kind == "qkv":
                            last = nc.tensor.matmul(bank[:, t * W:(t + 1) * W], x_cur[par][:, tile * P:(tile + 1) * P],
                                                    w_cur[par][:, :], start=True, stop=True)
                            continue
                        if kind == "out":
                            src = pv_sb[:, t * P:(t + 1) * P]
                        else:
                            st = stage[par if kind != "shift" or part == 1 else 1 - par]
                            heads = slice(J, 2 * J) if kind == "k" else slice(0, J)
                            src = st[:, tile, heads, :].rearrange("p j r -> p (j r)").bitcast(F32)
                        last = nc.tensor.transpose(bank[:, t * P:(t + 1) * P], src, ident[:, :])
                    last.then_inc(round_full, 1)

            def body(n, par):
                a, m, f = has(n)
                for s in range(SLOTS + 1):
                    if a and s < SLOTS:
                        score(n, par, s)
                    if m and s % 2 == 1:
                        maxima(n + 1, 1 - par, s // 2)
                    if a and s % J == 1 and s > J:
                        weigh(n, par, s // J - 1)
                    if a and s == SLOTS:
                        weigh(n, par, GROUPS - 1)
                    rounds(n, par, s)

            items(pe, body)

        @block.scalar
        def _(act):
            act.sem_inc(exp_ok, 2)

            def soften(n, par, s):
                qh, kt, j = s // (KT * J), s // J % KT, s % J
                if j == 0:
                    act.wait_ge(pv_ok, GROUPS * n + s // J + 1)
                act.wait_ge(s_full, SLOTS * n + s + 1)
                nc.scalar.activation(prob[s // J % 2][:, j, :], s_ps[s % 2][:, :], ACT.Exp, scale=SCALE)\
                  .then_inc(exp_ok, 1)

            def rounds(n, par, slot):
                for kind, part, r in at(n, slot):
                    if kind == "qkv" and part == 1:
                        act.wait_ge(pre_ok, 2 * (n + 3))
                        nc.scalar.activation(expd[:, :, :], pre[:, :, 0:2 * GF], ACT.Exp).then_inc(exp_f_ok, 1)
                    if kind in ("k", "q", "shift"):
                        act.wait_ge(round_full, r + 1)
                        other = kind == "shift" and part == 0
                        dst = {"k": k_raw, "q": q_raw, "shift": q_sh}[kind][1 - par if other else par]
                        if kind == "k" and has(n)[0]:
                            act.wait_ge(max_full, PAIRS * (n + 1))
                            act.wait_ge(kmask_in[par], 16 * J * (n // 2 + 1))
                        if kind == "q" and has(n)[0]:
                            act.wait_ge(qmask_in[par], 16 * J * (n // 2 + 1))
                        nc.scalar.activation(dst[:, part * CH:(part + 1) * CH], bank[:, :], ACT.Copy)\
                          .then_inc(q_sh_ok if kind == "shift" else raw_ok, 1)
                        done = (2 * (n + (part == 0)) + part + 1) if kind == "shift" \
                            else 4 * (n + 2) + 2 * (kind == "q") + part + 1
                        act.wait_ge(q_sh_ok if kind == "shift" else raw_ok, done)
                        act.sem_inc(round_free, 1)

            def body(n, par):
                a, m, f = has(n)
                for s in range(SLOTS + 1):
                    if a and s < SLOTS:
                        soften(n, par, s)
                    rounds(n, par, s)

            items(act, body)

        @block.vector
        def _(dve):
            dve.sem_inc(max_ok, 2)
            dve.sem_inc(round_free, 1)
            dve.sem_inc(pv_out, 1)
            for i in range(2):
                nc.vector.memset(stage[i][:, :, :, SHIFT:ROWS].bitcast(F32), 0.0).then_inc(ready, 1)
            nc.vector.memset(q_mask[0][:, :, :].bitcast(F32), 0.0)
            for i in range(2):
                nc.vector.memset(k_mask[i][:, :, :].bitcast(F32), 0.0)
            dve.wait_ge(ready, 3)
            for i in range(2):
                nc.vector.memset(stage[i][:, :, J:2 * J, SHIFT:SHIFT + 2].bitcast(F32), 1.0)
                nc.vector.memset(v_st[i][:, :, :, D:D + 1], 1.0).then_inc(ready, 1)

            def largest(m, par, k):
                qt, j = k // J, k % J
                dve.wait_ge(max_full, PAIRS * m + k + 1)
                nc.vector.tensor_reduce(out=neg_max[par][:, qt, j, :], in_=m_ps[k % 2][:, :], axis=AX.X, op=ALU.max,
                                        negate=True)\
                   .then_inc(max_ok, 1)

            def rounds(n, par, slot):
                for kind, part, r in at(n, slot):
                    if kind == "qkv":
                        dve.wait_ge(round_full, r + 1)
                        f = n + 2
                        if part == 0 and not (type(n) is int and n < -1):
                            dve.wait_ge(front_ok, 3 * f)
                        wide = bias[:, bass.ds(f % HG, 1), :].broadcast_to([P, CT, W])
                        nc.vector.tensor_tensor(pre[:, part * CT:(part + 1) * CT, :],
                                                bank[:, 0:CT * W].rearrange("p (t w) -> p t w", w=W),
                                                wide, ALU.add).then_inc(pre_ok, 1)
                        dve.wait_ge(pre_ok, 2 * f + part + 1)
                        dve.sem_inc(round_free, 1)
                    if kind == "out":
                        dve.wait_ge(round_full, r + 1)
                        v = bank[:, :].rearrange("p (t j r) -> p t j r", t=CT, r=ROWS)
                        nc.vector.reciprocal(r_sum[:, :, :, :], v[:, :, :, D:D + 1]).then_inc(rsum_ok, 1)
                        dve.wait_ge(rsum_ok, 2 * n + part + 1)
                        if not (type(n) is int and n == 0):
                            dve.wait_ge(res_ok, 2 * n)
                        nc.vector.tensor_tensor(attn[part][:, :, :, :], v[:, :, :, 0:D],
                                                r_sum[:, :, :, :].broadcast_to([P, CT, J, D]),
                                                ALU.mult).then_inc(attn_ok, 1)
                        dve.wait_ge(attn_ok, 2 * n + part + 1)
                        dve.sem_inc(round_free, 1)

            def take_values(n, h):
                dve.wait_ge(pv_ok, GROUPS * n + (h + 1) * KT + 2)
                nc.vector.tensor_copy(pv_sb[:, :], pv_ps[:, :]).then_inc(pv_out, 1)

            def body(n, par):
                a, m, f = has(n)
                for s in range(SLOTS + 1):
                    if m and s % 2 == 1:
                        largest(n + 1, 1 - par, s // 2)
                    if a and s in (SLOTS // 2 + 2, SLOTS):
                        take_values(n, s // SLOTS)
                    rounds(n, par, s)

            items(dve, body)


def build(nc, io):
    with ExitStack() as ctx:
        keep = {
            "ident": ctx.enter_context(nc.sbuf_tensor("ident", [P, P], F32)),
            "xnT": ctx.enter_context(nc.sbuf_tensor("xnT", [P, NTOK], F32)),
            "silu_t": ctx.enter_context(nc.sbuf_tensor("silu_t", [P, TILES, C], F32)),
        }
        io["gate_scratch"] = nc.dram_tensor("gate_scratch", [TILES * ER, P], F32).ap()
        io["rest_scratch"] = nc.dram_tensor("rest_scratch", [NTOK, C], F32).ap()
        with ExitStack() as c2:
            psum = [c2.enter_context(nc.psum_tensor(f"ps{i}", [P, 512], F32)) for i in range(8)]
            ffn = {k: c2.enter_context(nc.sbuf_tensor(k, [P, NTOK], F32R)) for k in ("xrh", "xrl")}
            ffn |= {k: c2.enter_context(nc.sbuf_tensor(k, [P, E, HID], F32R)) for k in ("w1h", "w1l", "w2h", "w2l")}
            prologue(nc, keep, ffn, io, psum)
            experts(nc, keep, ffn, io, psum)
        with ExitStack() as c3:
            def bank(name, n=1):
                return c3.enter_context(nc.psum_tensor(name, [P, 512 * n], F32))
            psum = {0: bank("s0"), 1: bank("s1"), "m0": bank("m0", 2), "m1": bank("m1", 2), 6: bank("pv"), 7: bank("sh")}
            attention(nc, keep, io, psum)


def kernel(**inputs):
    import numpy as np
    import concourse.bacc as bacc
    from concourse.bass_utils import run_bass_kernel_spmd

    a = {k[3:]: np.asarray(v) for k, v in inputs.items()}
    w = a["attn_w_qkv"].reshape(3, HG, GF, C)
    bq = a["attn_b_qkv"].reshape(3, HG, GF)

    def lay(x):
        return np.ascontiguousarray(x)

    w1 = np.concatenate([a["ffn_W1_s"], a["ffn_W1_r"]])
    w2 = np.concatenate([a["ffn_W2_s"], a["ffn_W2_r"]])
    b1 = np.concatenate([a["ffn_b1_s"], a["ffn_b1_r"]])
    b2 = np.concatenate([a["ffn_b2_s"], a["ffn_b2_r"]])
    pos = np.arange(T, dtype=np.float32)[:, None]
    div = np.exp(np.arange(0, D, 2, dtype=np.float32) * np.float32(-np.log(10000.0) / D)).astype(np.float32)
    ang = pos * div
    def table(f):
        return lay(f(ang).astype(np.float32).reshape(BT, P, D // 2).transpose(1, 0, 2))

    arrays = {
        "x": lay(a["attn_x"]),
        "ident": np.eye(P, dtype=np.float32),
        "rank": lay(np.broadcast_to(np.arange(ER, 0, -1, dtype=np.float32), (P, TILES, ER))),
        "cosine": table(np.cos),
        "sine": table(np.sin),
        "cent": lay(a["ffn_centroids"]),
        "gains": lay(np.stack([a["ffn_g_shared"]] * ES + [a["ffn_g_routed"]] * ER, axis=1)),
        "w1": lay(w1.transpose(1, 0, 2)),
        "w2": lay(w2.reshape(E, HT, P, C).transpose(2, 0, 1, 3).reshape(P, E, HID)),
        "b1": lay(b1.reshape(E * HT, P).T),
        "b2": lay(b2.T),
        "wv": lay(w[2].reshape(C, C).T),
        "cols": lay(np.concatenate([a["attn_w_lepe"][:, 0, :], a["attn_b_lepe"][:, None],
                                    a["attn_b_qkv"][2 * C:, None]], axis=1)),
        "wqkv": lay(w.transpose(3, 1, 0, 2).reshape(C, HG, 3 * GF)),
        "bqkv": lay(np.broadcast_to(bq.transpose(1, 0, 2).reshape(1, HG, 3 * GF), (P, HG, 3 * GF))),
    }
    nc = bacc.Bacc("TRN2", target_bir_lowering=False, num_devices=1)
    io = {k: nc.dram_tensor(f"in_{k}", v.shape, mybir.dt.from_np(v.dtype), kind="ExternalInput").ap()
          for k, v in arrays.items()}
    io["out"] = nc.dram_tensor("out", (B, T, C), F32, kind="ExternalOutput").ap()
    build(nc, io)
    r = run_bass_kernel_spmd(nc, [{f"in_{k}": v for k, v in arrays.items()}], core_ids=[0])
    return r.results[0]["out"]
```

```python
import concourse.bass as bass
from concourse import mybir
from contextlib import ExitStack

P = 128
C = 128
B, T = 4, 1024
NTOK = B * T
TILES = NTOK // P
BT = T // P
H, D = 16, 8
HG, J = 4, 4
GF = J * D
HID = 512
HT = HID // P
ES, ER = 2, 8
E = ES + ER
CH = 512
NCH = NTOK // CH
CT = CH // P
SCALE = float(D) ** -0.5
LN_EPS = 1e-5
RMS_EPS = 1.1920929e-07

F32 = mybir.dt.float32
F32R = mybir.dt.float32r
ALU = mybir.AluOpType
ACT = mybir.ActivationFunctionType
AX = mybir.AxisListType


def wait_apart(eng, sem, value, passed):
    eng.wait_ge(sem, value)
    eng.sem_inc(passed, 1)


class Chain:

    def __init__(self, eng, sem, base=0, passed=None):
        self.eng, self.sem, self.base, self.n, self.passed = eng, sem, base, 0, passed

    def did(self, ins):
        ins.then_inc(self.sem, 1)
        self.n += 1
        return ins

    def settle(self, apart=False):
        self.eng.wait_ge(self.sem, self.base + self.n)
        if apart:
            self.eng.sem_inc(self.passed, 1)


def prologue(nc, keep, ffn, io, psum):
    QT = BT
    EH = E // 2
    STEPS = 6
    with ExitStack() as ctx:
        def sb(name, shape, dt=F32):
            return ctx.enter_context(nc.sbuf_tensor(name, shape, dt))

        def sem(name):
            return ctx.enter_context(nc.semaphore(name))

        x_q = sb("x_q", [P, B, QT, C])
        xn_q = [sb(f"xn_q{i}", [P, QT, C]) for i in range(2)]
        xr_q = [sb(f"xr_q{i}", [P, QT, C]) for i in range(2)]
        w1_in = sb("w1_in", [P, EH, HID])
        w2_in = sb("w2_in", [P, EH, HID])
        gains = sb("gains", [P, E])
        cent = sb("cent", [P, ER])
        rank = sb("rank", [P, TILES, ER])
        st = sb("st", [P, QT, 6])
        mv = sb("mv", [P, QT, 2])
        var_eps = sb("var_eps", [P, QT])
        sd = sb("sd", [P, QT])
        rstd = sb("rstd", [P, QT])
        rvar = sb("rvar", [P, QT])
        ms = sb("ms", [P, QT])
        ms_eps = sb("ms_eps", [P, QT])
        rms = sb("rms", [P, QT])
        rrms = sb("rrms", [P, QT])
        th = sb("th", [P, TILES, ER])
        score = sb("score", [P, TILES, ER])
        left = sb("left", [P, TILES, ER])
        hit = sb("hit", [P, TILES, ER])
        pick = [sb(f"pick{i}", [P, TILES, ER]) for i in range(2)]
        best = sb("best", [P, TILES])
        total = sb("total", [P, TILES])
        rtotal = sb("rtotal", [P, TILES])
        gate = sb("gate", [P, TILES, ER])
        gateT = sb("gateT", [P, 2, P])

        tr_n = [psum[0], psum[1]]
        tr_r = [psum[2], psum[3]]
        logit = psum[4]
        tr_g = psum[5]

        const_in = sem("p_const_in")
        ffn_in = sem("p_ffn_in")
        passed = sem("p_passed")
        x_in = [sem(f"p_x_in{i}") for i in range(2)]
        w1_ld = sem("p_w1_in")
        w2_ld = sem("p_w2_in")
        w1_used = sem("p_w1_used")
        w2_used = sem("p_w2_used")
        w2_hi = sem("p_w2_hi")
        w1_hi = sem("p_w1_hi")
        own = sem("p_own")
        route = sem("p_route")
        var_ok = sem("p_var_ok")
        sd_ok = sem("p_sd_ok")
        xn_ok = sem("p_xn_ok")
        ms_ok = sem("p_ms_ok")
        rms_ok = sem("p_rms_ok")
        rrms_ok = sem("p_rrms_ok")
        xr_ok = sem("p_xr_ok")
        xr_hi = sem("p_xr_hi")
        xnT_full = sem("p_xnT_full")
        xnT_out = sem("p_xnT_out")
        xrT_full = sem("p_xrT_full")
        xrT_out = sem("p_xrT_out")
        logit_ok = sem("p_logit_ok")
        th_ok = sem("p_th_ok")
        gate_ok = sem("p_gate_ok")
        gateT_full = sem("p_gateT_full")
        gateT_ok = sem("p_gateT_ok")
        gateT_st = sem("p_gateT_st")

        ident = keep["ident"]
        xnT = keep["xnT"]
        block = ctx.enter_context(nc.Block())

        @block.sync
        def _(sp):
            x_v = io["x"].rearrange("b (t p) c -> b p t c", p=P)
            for i in range(2):
                sp.dma_start(x_q[:, i, :, :], x_v[i, :, :, :]).then_inc(x_in[i], 16)
                if i == 0:
                    sp.dma_start(ident[:, :], io["ident"]).then_inc(const_in, 16)
                    sp.dma_start(gains[:, :], io["gains"]).then_inc(const_in, 16)
                    sp.dma_start(cent[:, :], io["cent"]).then_inc(const_in, 16)
                    sp.dma_start(rank[:, :, :], io["rank"]).then_inc(const_in, 16)
                    sp.dma_start(w2_in[:, :, :], io["w2"][:, 0:EH, :]).then_inc(w2_ld, 16)
            sp.dma_start(w1_in[:, :, :], io["w1"][:, 0:EH, :]).then_inc(w1_ld, 16)
            for i in range(2):
                sp.wait_ge(x_in[i], 16)
                sp.dma_start(x_q[:, 2 + i, :, :], x_v[2 + i, :, :, :]).then_inc(x_in[i], 16)
            for k in ("b1", "b2", "wv", "cols"):
                sp.dma_start(ffn[k][:, :], io[k]).then_inc(ffn_in, 16)
            sp.wait_ge(w2_used, EH)
            sp.dma_start(w2_in[:, :, :], io["w2"][:, EH:E, :]).then_inc(w2_ld, 16)
            sp.wait_ge(w1_used, EH)
            sp.dma_start(w1_in[:, :, :], io["w1"][:, EH:E, :]).then_inc(w1_ld, 16)
            sp.wait_ge(gateT_ok, 1)
            for h in range(2):
                sp.dma_start(io["gate_scratch"][h * P:(h + 1) * P, :], gateT[:, h, :]).then_inc(gateT_st, 16)
            sp.wait_ge(gateT_st, 32)
            sp.wait_ge(ffn_in, 64)

        @block.gpsimd
        def _(pool):
            for h in range(2):
                pool.wait_ge(w2_ld, 16 * (h + 1))
                with pool.Fori(0, EH) as k:
                    whole = w2_in[:, bass.ds(k, 1), :].rearrange("p a n -> p (a n)")
                    hi, lo = (m[:, bass.ds(k + h * EH, 1), :].rearrange("p a n -> p (a n)")
                              for m in (ffn["w2h"], ffn["w2l"]))
                    nc.gpsimd.tensor_copy(hi, whole).then_inc(w2_hi, 1)
                    pool.wait_ge(w2_hi, k + h * EH + 1)
                    nc.gpsimd.tensor_tensor(lo, whole, hi.bitcast(F32), ALU.subtract).then_inc(w2_used, 1)

        @block.vector
        def _(dve):
            dve.sem_inc(xrT_out, 2)

            def batch(b, i, pair):
                own_steps = Chain(dve, own, b * STEPS, passed)
                xb = x_q[:, bass.ds(b, 1), :, :].rearrange("p a t c -> p (a t) c")
                dve.wait_ge(x_in[i], 16 * (pair + 1))
                for t in range(QT):
                    last = nc.vector.bn_stats(st[:, t, :], xb[:, t, :])
                own_steps.did(last)
                if not (type(b) is int and b == 0):
                    low_parts(b - 1)
                own_steps.settle(apart=True)
                for t in range(QT):
                    last = nc.vector.bn_aggr(mv[:, t, :], st[:, t, :])
                own_steps.did(last)
                own_steps.settle()
                nc.vector.tensor_scalar(var_eps[:, :], mv[:, :, 1], LN_EPS, None, ALU.add).then_inc(var_ok, 1)
                dve.wait_ge(var_ok, b + 1)
                own_steps.did(nc.vector.reciprocal(rvar[:, :], var_eps[:, :]))
                own_steps.settle()
                own_steps.did(nc.vector.tensor_tensor(ms[:, :], mv[:, :, 1], rvar[:, :], ALU.mult))
                own_steps.settle()
                nc.vector.tensor_scalar(ms_eps[:, :], ms[:, :], RMS_EPS, None, ALU.add).then_inc(ms_ok, 1)
                dve.wait_ge(sd_ok, b + 1)
                own_steps.did(nc.vector.reciprocal(rstd[:, :], sd[:, :]))
                dve.wait_ge(rms_ok, b + 1)
                own_steps.did(nc.vector.reciprocal(rrms[:, :], rms[:, :]))
                own_steps.settle()
                dve.sem_inc(rrms_ok, 1)
                dve.wait_ge(xnT_full, 2 * b + 2)
                for t in range(QT):
                    nc.vector.tensor_scalar(xn_q[i][:, t, :], xb[:, t, :], mv[:, t, 0:1], rstd[:, t:t + 1],
                                            ALU.subtract, ALU.mult).then_inc(xn_ok, 1)
                assert own_steps.n == STEPS

            def low_parts(b):
                for h in range(2):
                    cols = bass.ds(b * T + h * CH, CH)
                    dve.wait_ge(xr_hi, 2 * b + h + 1)
                    nc.vector.tensor_tensor(ffn["xrl"][:, cols], tr_r[h][:, :],
                                            ffn["xrh"][:, cols].bitcast(F32), ALU.subtract).then_inc(xrT_out, 1)

            def first_lows(h):
                for k in range(EH):
                    e = h * EH + k
                    dve.wait_ge(w1_hi, e + 1)
                    nc.vector.scalar_tensor_tensor(ffn["w1l"][:, e, :], w1_in[:, k, :], gains[:, e:e + 1],
                                                   ffn["w1h"][:, e, :].bitcast(F32),
                                                   ALU.mult, ALU.subtract).then_inc(w1_used, 1)

            batch(0, 0, 0)
            batch(1, 1, 0)
            batch(2, 0, 1)
            first_lows(0)
            batch(3, 1, 1)
            low_parts(3)
            first_lows(1)

            def wide(m):
                return m.rearrange("p (t a) -> p t a", a=1).broadcast_to([P, TILES, ER])

            r = Chain(dve, route)
            dve.wait_ge(th_ok, 1)
            r.did(nc.vector.tensor_scalar(score[:, :, :], th[:, :, :], 0.5, 0.5, ALU.mult, ALU.add))
            r.settle()
            r.did(nc.vector.reduce_sum(total[:, :], score[:, :, :], axis=AX.X))
            r.settle()
            r.did(nc.vector.reciprocal(rtotal[:, :], total[:, :]))
            for k in range(2):
                src = score if k == 0 else left
                r.did(nc.vector.reduce_max(best[:, :], src[:, :, :], axis=AX.X))
                r.settle()
                r.did(nc.vector.tensor_tensor(hit[:, :, :], src[:, :, :], wide(best[:, :]), ALU.is_ge))
                r.settle()
                r.did(nc.vector.tensor_tensor(hit[:, :, :], hit[:, :, :], rank[:, :, :], ALU.mult))
                r.settle()
                r.did(nc.vector.reduce_max(best[:, :], hit[:, :, :], axis=AX.X))
                r.settle()
                r.did(nc.vector.tensor_tensor(pick[k][:, :, :], hit[:, :, :], wide(best[:, :]), ALU.is_equal))
                r.settle()
                if k == 0:
                    r.did(nc.vector.scalar_tensor_tensor(left[:, :, :], pick[0][:, :, :], -4.0, score[:, :, :],
                                                         ALU.mult, ALU.add))
                    r.settle()
            r.did(nc.vector.tensor_tensor(pick[0][:, :, :], pick[0][:, :, :], pick[1][:, :, :], ALU.add))
            r.settle()
            r.did(nc.vector.tensor_tensor(gate[:, :, :], pick[0][:, :, :], score[:, :, :], ALU.mult))
            r.settle()
            nc.vector.tensor_tensor(gate[:, :, :], gate[:, :, :], wide(rtotal[:, :]), ALU.mult).then_inc(gate_ok, 1)
            dve.wait_ge(gateT_full, 2)
            nc.vector.tensor_copy(gateT[:, :, :].rearrange("p h n -> p (h n)"), tr_g[:, 0:2 * P]).then_inc(gateT_ok, 1)

        @block.scalar
        def _(act):
            act.sem_inc(xnT_out, 2)

            def first_matrix(k, h):
                e = h * EH + k
                nc.scalar.activation(ffn["w1h"][:, bass.ds(e, 1), :].rearrange("p a n -> p (a n)"), w1_in[:, k, :],
                                     ACT.Copy, scale=gains[:, bass.ds(e, 1)]).then_inc(w1_hi, 1)

            with act.Fori(0, B // 2) as pair:
                for i in range(2):
                    b = pair * 2 + i
                    act.wait_ge(var_ok, b + 1)
                    nc.scalar.activation(sd[:, :], var_eps[:, :], ACT.Sqrt).then_inc(sd_ok, 1)
                    act.wait_ge(ms_ok, b + 1)
                    nc.scalar.activation(rms[:, :], ms_eps[:, :], ACT.Sqrt).then_inc(rms_ok, 1)
                    act.wait_ge(rrms_ok, b + 1)
                    for t in range(QT):
                        act.wait_ge(xn_ok, QT * b + t + 1)
                        nc.scalar.activation(xr_q[i][:, t, :], xn_q[i][:, t, :], ACT.Copy,
                                             scale=rrms[:, t:t + 1]).then_inc(xr_ok, 1)
                    for h in range(2):
                        act.wait_ge(xnT_full, 2 * b + h + 1 + 4)
                        nc.scalar.activation(xnT[:, bass.ds(b * T + h * CH, CH)], tr_n[h][:, :],
                                             ACT.Copy).then_inc(xnT_out, 1)
                    for h in range(2):
                        act.wait_ge(xrT_full, 2 * b + h + 1)
                        nc.scalar.activation(ffn["xrh"][:, bass.ds(b * T + h * CH, CH)], tr_r[h][:, :],
                                             ACT.Copy).then_inc(xr_hi, 1)
                    if i == 1:
                        act.wait_ge(w1_ld, 16 * (pair + 1))
                        act.wait_ge(const_in, 64)
                        for k in range(EH):
                            first_matrix(k, pair)
            act.wait_ge(logit_ok, 1)
            nc.scalar.activation(th[:, :, :], logit[:, 0:TILES * ER].rearrange("p (t e) -> p t e", e=ER),
                                 ACT.Tanh, scale=0.5).then_inc(th_ok, 1)

        @block.tensor
        def _(pe):
            pe.wait_ge(const_in, 64)
            pe.sem_inc(xnT_full, 4)
            for b in range(B):
                i = b % 2
                for h in range(2):
                    pe.wait_ge(xn_ok, QT * b + 4 * (h + 1))
                    pe.wait_ge(xnT_out, 2 * b + 2)
                    for k in range(4):
                        last = nc.tensor.transpose(tr_n[h][:, k * P:(k + 1) * P], xn_q[i][:, 4 * h + k, :],
                                                   ident[:, :])
                    last.then_inc(xnT_full, 1)
                for h in range(2):
                    pe.wait_ge(xr_ok, QT * b + 4 * (h + 1))
                    pe.wait_ge(xrT_out, 2 * b + 2)
                    for k in range(4):
                        last = nc.tensor.transpose(tr_r[h][:, k * P:(k + 1) * P], xr_q[i][:, 4 * h + k, :],
                                                   ident[:, :])
                    last.then_inc(xrT_full, 1)
                pe.wait_ge(xnT_out, 2 * b + 4)
                for t in range(b * BT, (b + 1) * BT):
                    last = nc.tensor.matmul(logit[:, t * ER:(t + 1) * ER], xnT[:, t * P:(t + 1) * P], cent[:, :],
                                            start=True, stop=True)
            last.then_inc(logit_ok, 1)
            pe.wait_ge(gate_ok, 1)
            flat = gate[:, :, :].rearrange("p t e -> p (t e)")
            for h in range(2):
                nc.tensor.transpose(tr_g[:, h * P:(h + 1) * P], flat[:, h * P:(h + 1) * P],
                                    ident[:, :]).then_inc(gateT_full, 1)


def experts(nc, keep, ffn, io, psum):
    NQ = E * HT
    NY = 1 + ER
    LAG = 3
    HB = 4
    TAIL_AT, CONV_AT = 10, 22
    with ExitStack() as ctx:
        def sb(name, shape, dt=F32):
            return ctx.enter_context(nc.sbuf_tensor(name, shape, dt))

        def sem(name):
            return ctx.enter_context(nc.semaphore(name))

        hidden = [sb(f"hidden{i}", [P, CH]) for i in range(2)]
        hid_hi = [sb(f"hid_hi{i}", [P, CH], F32R) for i in range(HB)]
        hid_lo = [sb(f"hid_lo{i}", [P, CH], F32R) for i in range(HB)]
        gates = [sb(f"gates{i}", [P, CH]) for i in range(2)]
        gated = [sb(f"gated{i}", [P, CH]) for i in range(2)]
        acc = [sb(f"acc{i}", [P, CH]) for i in range(2)]
        tanh_g = sb("tanh_g", [P, CH])
        silu_g = sb("silu_g", [P, CH])
        lepe_g = sb("lepe_g", [P, CH])
        x_c = sb("x_c", [P, CT, C])
        rest = sb("rest", [P, CT, C])
        v_pad = sb("v_pad", [P, T + 2])
        lepe = sb("lepe", [P, T])
        b2s = sb("b2s", [P, 1])

        hid_ps = psum[0:HB]
        y_ps = psum[4:6]
        aux = [psum[6], psum[7]]

        passed = sem("f_passed")
        ready = sem("f_ready")
        hid_full = sem("f_hid_full")
        gelu_ok = sem("f_gelu_ok")
        hi_ok = sem("f_hi_ok")
        split_ok = sem("f_split_ok")
        down_ok = sem("f_down_ok")
        y_out = sem("f_y_out")
        gates_in = [sem(f"f_gates_in{i}") for i in range(2)]
        acc_ok = sem("f_acc_ok")
        tanh_ok = sem("f_tanh_ok")
        pool_own = sem("f_pool_own")
        tail_ok = sem("f_tail_ok")
        aux_full = sem("f_aux_full")
        silu_out = sem("f_silu_out")
        rest_ok = sem("f_rest_ok")
        x_c_in = sem("f_x_c_in")
        rest_st = sem("f_rest_st")
        v_full = sem("f_v_full")
        v_ok = sem("f_v_ok")
        conv_own = sem("f_conv_own")
        conv_ok = sem("f_conv_ok")

        ident, xnT, silu_t = keep["ident"], keep["xnT"], keep["silu_t"]
        b1, b2, wv, cols = (ffn[k] for k in ("b1", "b2", "wv", "cols"))
        block = ctx.enter_context(nc.Block())

        def chunks(eng, body):
            body(0, 0, False)
            with eng.Fori(0, (NCH - 2) // 2) as pair:
                body(pair * 2 + 1, 1, True)
                body(pair * 2 + 2, 0, True)
            body(NCH - 1, 1, True)

        def gate_slot(y):
            return (y - 1) % 2

        @block.sync
        def _(sp):
            gate_v = io["gate_scratch"].rearrange("(c t e) n -> c e t n", t=CT, e=ER)
            x_v = io["x"].rearrange("b (h t p) c -> (b h) p t c", p=P, t=CT)
            rest_v = io["rest_scratch"].rearrange("(c t p) n -> c p t n", p=P, t=CT)

            def load_x(c):
                sp.dma_start(x_c[:, :, :], x_v[bass.ds(c, 1), :, :, :].rearrange("a p t c -> p (a t) c"))\
                  .then_inc(x_c_in, 16)

            def store_rest(c):
                wait_apart(sp, rest_ok, c + 1, passed)
                sp.dma_start(rest_v[bass.ds(c, 1), :, :, :].rearrange("a p t c -> p (a t) c"), rest[:, :, :])\
                  .then_inc(rest_st, 16)

            def body(c, par, tail):
                for y in range(1, NY):
                    wait_apart(sp, y_out, c * NY + (y if y <= 2 else y + 1), passed)
                    src = gate_v[bass.ds(c, 1), y - 1, :, :]
                    sp.dma_start(gates[gate_slot(y)][:, :].rearrange("p (t n) -> p t n", n=P),
                                 src.broadcast_to([P, CT, P])).then_inc(gates_in[gate_slot(y)], 16)
                    if y == 4 and tail:
                        store_rest(c - 1)
                        load_x(c)

            sp.sem_inc(rest_st, 16)
            load_x(0)
            chunks(sp, body)
            store_rest(NCH - 1)
            sp.wait_ge(rest_st, 16 * (NCH + 1))

        @block.tensor
        def _(pe):
            pe.sem_inc(down_ok, HB)
            pe.sem_inc(aux_full, 2)

            def up(c, q):
                e, ht = q // HT, q % HT
                toks = bass.ds(c * CH, CH)
                m = slice(ht * P, (ht + 1) * P)
                bank = hid_ps[q % HB]
                pe.wait_ge(gelu_ok, c * NQ + q + 1)
                nc.tensor.matmul(bank[:, :], ffn["w1h"][:, e, m], ffn["xrh"][:, toks], start=True, stop=False)
                nc.tensor.matmul(bank[:, :], ffn["w1h"][:, e, m], ffn["xrl"][:, toks], start=False, stop=False)
                nc.tensor.matmul(bank[:, :], ffn["w1l"][:, e, m], ffn["xrh"][:, toks], start=False, stop=True)\
                  .then_inc(hid_full, 1)

            def down(c, par, q):
                e, ht = q // HT, q % HT
                y = max(0, e - ES + 1)
                first, last = q in (0, *range(ES * HT, NQ, HT)), ht == HT - 1 and e >= ES - 1
                bank = y_ps[(par + y) % 2]
                m = slice(ht * P, (ht + 1) * P)
                if first:
                    pe.wait_ge(y_out, c * NY + y + 1)
                pe.wait_ge(split_ok, c * NQ + q + 1 + 2)
                nc.tensor.matmul(bank[:, :], ffn["w2h"][:, e, m], hid_hi[q % HB][:, :], start=first, stop=False)
                nc.tensor.matmul(bank[:, :], ffn["w2l"][:, e, m], hid_hi[q % HB][:, :], start=False, stop=False)
                nc.tensor.matmul(bank[:, :], ffn["w2h"][:, e, m], hid_lo[q % HB][:, :], start=False, stop=last)\
                  .then_inc(down_ok, 1)

            def tail_transposes(c):
                pe.wait_ge(tail_ok, c + 1)
                pe.wait_ge(v_ok, 2 * (c // 2) + 2)
                for bank, src in ((aux[0], silu_g), (aux[1], lepe_g)):
                    for t in range(CT):
                        last = nc.tensor.transpose(bank[:, t * P:(t + 1) * P], src[:, t * P:(t + 1) * P], ident[:, :])
                    last.then_inc(aux_full, 1)

            def v_product(b, after):
                pe.wait_ge(silu_out, after)
                pe.wait_ge(rest_ok, after)
                for h in range(2):
                    nc.tensor.matmul(aux[h][:, :], wv[:, :], xnT[:, bass.ds(b * T + h * CH, CH)],
                                     start=True, stop=True).then_inc(v_full, 1)

            def body(c, par, tail):
                for q in range(NQ + LAG):
                    if q < NQ:
                        up(c, q)
                    if q == TAIL_AT and tail:
                        tail_transposes(c - 1)
                    if q == CONV_AT and par == 0:
                        v_product(c // 2, c)
                    if q >= LAG:
                        down(c, par, q - LAG)

            chunks(pe, body)
            tail_transposes(NCH - 1)

        @block.scalar
        def _(act):
            act.sem_inc(gelu_ok, HB)

            def tanh_part(c, par):
                act.wait_ge(acc_ok, (c + 1) * ER)
                nc.scalar.activation(tanh_g[:, :], acc[par][:, :], ACT.Tanh, scale=0.5).then_inc(tanh_ok, 1)

            def silu_part(c):
                act.wait_ge(aux_full, 2 * c + 1 + 2)
                nc.scalar.activation(silu_t[:, bass.ds(c * CT, CT), :],
                                     aux[0][:, :].rearrange("p (t n) -> p t n", n=P), ACT.Copy).then_inc(silu_out, 1)

            def body(c, par, tail):
                for q in range(NQ):
                    act.wait_ge(hid_full, c * NQ + q + 1)
                    act.wait_ge(split_ok, c * NQ + q + 1)
                    nc.scalar.activation(hidden[q % 2][:, :], hid_ps[q % HB][:, :], ACT.Gelu,
                                         bias=b1[:, q:q + 1]).then_inc(gelu_ok, 1)
                    if q == 3 and tail:
                        tanh_part(c - 1, 1 - par)
                    if q == TAIL_AT + 1 and tail:
                        silu_part(c - 1)
                    if q == CONV_AT + 1 and par == 0:
                        for h in range(2):
                            act.wait_ge(v_full, c + h + 1)
                            act.wait_ge(conv_ok, c // 2 + 1)
                            nc.scalar.activation(v_pad[:, 1 + h * CH:1 + (h + 1) * CH], aux[h][:, :],
                                                 ACT.Identity, bias=cols[:, 4:5]).then_inc(v_ok, 1)

            chunks(act, body)
            tanh_part(NCH - 1, 1)
            silu_part(NCH - 1)

        @block.vector
        def _(dve):
            dve.sem_inc(split_ok, 2)
            dve.sem_inc(y_out, 2)
            dve.sem_inc(conv_ok, 1)
            nc.vector.memset(v_pad[:, 0:1], 0.0)
            nc.vector.memset(v_pad[:, T + 1:T + 2], 0.0).then_inc(ready, 1)
            nc.vector.tensor_tensor(b2s[:, :], b2[:, 0:1], b2[:, 1:2], ALU.add).then_inc(ready, 1)
            dve.wait_ge(ready, 2)

            def split(c, q):
                dve.wait_ge(gelu_ok, c * NQ + q + 1 + HB)
                dve.wait_ge(down_ok, c * NQ + q + 1)
                nc.vector.tensor_copy(hid_hi[q % HB][:, :], hidden[q % 2][:, :]).then_inc(hi_ok, 1)
                dve.wait_ge(hi_ok, c * NQ + q + 1)
                nc.vector.tensor_tensor(hid_lo[q % HB][:, :], hidden[q % 2][:, :], hid_hi[q % HB][:, :].bitcast(F32),
                                        ALU.subtract).then_inc(split_ok, 1)

            def output(c, par, y):
                dve.wait_ge(down_ok, c * NQ + (ES + y) * HT + HB)
                bank = y_ps[(par + y) % 2]
                if y == 0:
                    nc.vector.scalar_tensor_tensor(acc[par][:, :], bank[:, :], b2s[:, 0:1],
                                                   xnT[:, bass.ds(c * CH, CH)], ALU.add, ALU.add)\
                      .then_inc(y_out, 1)
                    return
                slot = gate_slot(y)
                dve.wait_ge(gates_in[slot], 16 * (ER // 2) * c + 16 * ((y - 1) // 2 + 1))
                if y > 2 or not (type(c) is int and c == 0):
                    dve.wait_ge(acc_ok, c * ER + y - 2)
                nc.vector.scalar_tensor_tensor(gated[slot][:, :], bank[:, :], b2[:, ES + y - 1:ES + y],
                                               gates[slot][:, :], ALU.add, ALU.mult).then_inc(y_out, 1)

            def rest_part(c):
                dve.wait_ge(aux_full, 2 * c + 2 + 2)
                dve.wait_ge(x_c_in, 16 * (c + 1))
                dve.wait_ge(rest_st, 16 * (c + 1))
                nc.vector.tensor_tensor(rest[:, :, :], aux[1][:, :].rearrange("p (t n) -> p t n", n=P),
                                        x_c[:, :, :], ALU.add).then_inc(rest_ok, 1)

            def convolve(b, tails):
                dve.wait_ge(v_ok, 2 * b + 2)
                dve.wait_ge(tail_ok, tails)
                nc.vector.tensor_scalar(lepe[:, :], v_pad[:, 1:T + 1], cols[:, 1:2], cols[:, 3:4],
                                        ALU.mult, ALU.add).then_inc(conv_own, 1)
                dve.wait_ge(conv_own, 2 * b + 1)
                nc.vector.scalar_tensor_tensor(lepe[:, :], v_pad[:, 0:T], cols[:, 0:1], lepe[:, :],
                                               ALU.mult, ALU.add).then_inc(conv_own, 1)
                dve.wait_ge(conv_own, 2 * b + 2)
                nc.vector.scalar_tensor_tensor(lepe[:, :], v_pad[:, 2:T + 2], cols[:, 2:3], lepe[:, :],
                                               ALU.mult, ALU.add).then_inc(conv_ok, 1)

            def body(c, par, tail):
                for q in range(NQ):
                    split(c, q)
                    if q == TAIL_AT + 2 and tail:
                        rest_part(c - 1)
                    if q == CONV_AT + 3 and par == 0:
                        convolve(c // 2, c)
                    e, ht = (q - LAG - 1) // HT, (q - LAG - 1) % HT
                    if q > LAG and ht == HT - 1 and e >= ES - 1:
                        output(c, par, e - ES + 1)
                output(c, par, NY - 1)

            chunks(dve, body)
            rest_part(NCH - 1)

        @block.gpsimd
        def _(pool):
            def add(c, par, y):
                pool.wait_ge(y_out, c * NY + y + 1 + 2)
                pool.wait_ge(acc_ok, c * ER + y - 1)
                nc.gpsimd.tensor_tensor(acc[par][:, :], acc[par][:, :], gated[gate_slot(y)][:, :],
                                        ALU.add).then_inc(acc_ok, 1)

            def tail_part(c, par):
                wait_apart(pool, tanh_ok, c + 1, passed)
                own = Chain(pool, pool_own, 2 * c)
                own.did(nc.gpsimd.tensor_scalar(tanh_g[:, :], tanh_g[:, :], 0.5, 0.5, ALU.mult, ALU.add))
                own.settle()
                pool.wait_ge(aux_full, 2 * c + 2)
                own.did(nc.gpsimd.tensor_tensor(silu_g[:, :], acc[par][:, :], tanh_g[:, :], ALU.mult))
                own.settle()
                pool.wait_ge(conv_ok, c // 2 + 2)
                nc.gpsimd.tensor_tensor(lepe_g[:, :], lepe[:, par * CH:(par + 1) * CH], silu_g[:, :],
                                        ALU.mult).then_inc(tail_ok, 1)

            def body(c, par, tail):
                if tail:
                    tail_part(c - 1, 1 - par)
                for y in range(1, NY):
                    add(c, par, y)

            chunks(pool, body)
            tail_part(NCH - 1, 1)


def attention(nc, keep, io, psum):
    N = B * HG
    KT = T // P
    QH = T // CH
    SLOTS = QH * KT * J
    GROUPS = QH * KT
    HALVES = 2 * KT * J
    SB, MB = 3, 3
    W = 3 * GF
    ROWS = 32
    HI0, SECOND, THIRD, SHIFT = 0, D, 2 * D, 3 * D
    FRONT_ROUNDS, ROUNDS = 6, 10
    POOL_FRONT, POOL_MAX, POOL_OUT = 12, 2, 1
    POOL_STEPS = POOL_FRONT + QH * POOL_MAX + QH * POOL_OUT
    AT_SHIFT1, AT_QKV, AT_K, AT_Q, AT_SHIFT0, AT_LAST_OUT = 17, (9, 13), (41, 45), (49, 53), 61, 5

    with ExitStack() as ctx:
        def sb(name, shape, dt=F32):
            return ctx.enter_context(nc.sbuf_tensor(name, shape, dt))

        def sem(name):
            return ctx.enter_context(nc.semaphore(name))

        x_cur = [sb(f"x_cur{i}", [P, T]) for i in range(2)]
        w_cur = [sb(f"w_cur{i}", [P, W]) for i in range(2)]
        w_all = sb("w_all", [P, HG, W])
        bias = sb("bias", [P, HG, W])
        cosine = sb("cosine", [P, KT, D // 2])
        sine = sb("sine", [P, KT, D // 2])
        pre = sb("pre", [P, KT, W])
        expd = sb("expd", [P, KT, 2 * GF])
        feat = sb("feat", [P, KT, 2 * J, D])
        rope = [sb(f"rope{i}", [P, KT, 2 * J, D // 2]) for i in range(4)]
        turned = sb("turned", [P, KT, 2 * J, D])
        stage = [sb(f"stage{i}", [P, KT, 2 * J, ROWS], F32R) for i in range(2)]
        v_raw = [sb(f"v_raw{i}", [P, KT, J, D]) for i in range(2)]
        v_st = [sb(f"v_st{i}", [P, KT, J, ROWS]) for i in range(2)]
        k_raw = [sb(f"k_raw{i}", [P, T], F32R) for i in range(2)]
        q_raw = [sb(f"q_raw{i}", [P, T], F32R) for i in range(2)]
        k_mask = [sb(f"k_mask{i}", [P, J, T], F32R) for i in range(2)]
        q_mask = [sb(f"q_mask{i}", [P, J, T], F32R) for i in range(2)]
        q_sh = [sb(f"q_sh{i}", [P, T], F32R) for i in range(2)]
        neg_half = [sb(f"neg_half{i}", [P, KT, J, 2]) for i in range(2)]
        neg_max = sb("neg_max", [P, KT, J, 1])
        prob = [sb(f"prob{i}", [P, J, CH]) for i in range(2)]
        pv_sb = sb("pv_sb", [P, CH])
        r_sum = sb("r_sum", [P, CT, J, 1])
        attn = [sb(f"attn{i}", [P, CT, J, D]) for i in range(2)]
        rest = [sb(f"rest_a{i}", [P, KT, GF]) for i in range(2)]
        result = [sb(f"result{i}", [P, CT, GF]) for i in range(2)]

        s_ps = psum[0:SB]
        m_ps = psum[SB:SB + MB]
        pv_ps = psum[6]
        bank = psum[7]

        const_in = sem("a_const_in")
        passed = sem("a_passed")
        stage_ok = sem("a_stage_ok")
        v_pad_ok = sem("a_v_pad_ok")
        mask_ok = sem("a_mask_ok")
        q_mask1_ok = sem("a_q_mask1_ok")
        cur_ok = sem("a_cur_ok")
        round_full = sem("a_round_full")
        round_free = sem("a_round_free")
        pre_ok = sem("a_pre_ok")
        exp_f_ok = sem("a_exp_f_ok")
        pool_own = sem("a_pool_own")
        front_ok = sem("a_front_ok")
        raw_ok = sem("a_raw_ok")
        qmask_in = [sem(f"a_qmask_in{i}") for i in range(2)]
        kmask_in = [sem(f"a_kmask_in{i}") for i in range(2)]
        max_full = sem("a_max_full")
        max_ok = sem("a_max_ok")
        neg_ok = sem("a_neg_ok")
        shift_ok = sem("a_shift_ok")
        q_sh_ok = sem("a_q_sh_ok")
        v_st_ok = sem("a_v_st_ok")
        s_full = sem("a_s_full")
        exp_ok = sem("a_exp_ok")
        pv_ok = sem("a_pv_ok")
        pv_out = sem("a_pv_out")
        rsum_ok = sem("a_rsum_ok")
        attn_ok = sem("a_attn_ok")
        res_ok = sem("a_res_ok")
        rest_in = [sem(f"a_rest_in{i}") for i in range(2)]
        res_st = [sem(f"a_res_st{i}") for i in range(2)]

        ident, xnT, silu_t = keep["ident"], keep["xnT"], keep["silu_t"]
        block = ctx.enter_context(nc.Block())

        def items(eng, body):
            for n in (-2, -1, 0):
                body(n, n % 2)
            with eng.Fori(0, (N - 4) // 2) as pair:
                body(pair * 2 + 1, 1)
                body(pair * 2 + 2, 0)
            for n in range(N - 3, N + 1):
                body(n, n % 2)

        def has(n):
            if type(n) is not int:
                return True, True, True
            return 0 <= n < N, 0 <= n + 1 < N, n + 2 < N

        def after(n):
            return type(n) is not int or 1 <= n <= N

        def rounds_before(n):
            if type(n) is int and n < 1:
                return sum(len(schedule(i)) for i in range(-2, n))
            if type(n) is not int or n <= N - 2:
                return rounds_before(0) + ROUNDS * n - 1
            return rounds_before(n - 1) + len(schedule(n - 1))

        def schedule(n):
            a, m, f = has(n)
            out = []
            if f:
                out += [(AT_QKV[h], "qkv", h) for h in range(2)]
            if a:
                out += [(AT_SHIFT1, "shift", 1)]
            if a:
                out += [(SLOTS // 2 + 5, "out", 0)]
            if m:
                out += [(AT_SHIFT0, "shift", 0)]
            if f:
                out += [(AT_K[h], "k", h) for h in range(2)] + [(AT_Q[h], "q", h) for h in range(2)]
            if after(n):
                out += [(AT_LAST_OUT, "out", 1)]
            return [(*r, i) for i, r in enumerate(sorted(out, key=lambda r: r[0]))]

        def at(n, slot):
            return [(kind, part, rounds_before(n) + i) for s, kind, part, i in schedule(n) if s == slot]

        @block.sync
        def _(sp):
            for dst, src in ((w_all, "wqkv"), (bias, "bqkv"), (cosine, "cosine"), (sine, "sine")):
                sp.dma_start(dst[:, :, :], io[src]).then_inc(const_in, 16)
            rest_v = io["rest_scratch"].rearrange("(b t p) (g f) -> p b g t f", p=P, t=KT, f=GF)
            out_v = io["out"].rearrange("b (h t p) (g f) -> p b g h t f", p=P, t=CT, f=GF)

            def body(n, par):
                a, m, f = has(n)
                if a:
                    if not (type(n) is int and n < 2):
                        wait_apart(sp, res_ok, 2 * (n - 1) + 2, passed)
                    src = rest_v[:, bass.ds(n // HG, 1), bass.ds(n % HG, 1), :, :]
                    sp.dma_start(rest[par][:, :, :], src.rearrange("p b g t f -> p (b g t) f"))\
                      .then_inc(rest_in[par], 16)
                if m:
                    wait_apart(sp, raw_ok, 4 * (n + 2), passed)
                    if a:
                        sp.wait_ge(s_full, SLOTS * n)
                    if type(n) is int and n < 1:
                        sp.wait_ge(mask_ok, n + 3)
                    for j in range(J):
                        sp.dma_start(k_mask[1 - par][j * ROWS:(j + 1) * ROWS, j, :].bitcast(F32),
                                     k_raw[1 - par][j * ROWS:(j + 1) * ROWS, :].bitcast(F32)).then_inc(kmask_in[1 - par], 16)
                if after(n):
                    store(n - 1, 1)
                if a:
                    store(n, 0)
                if f:
                    wait_apart(sp, raw_ok, 4 * (n + 3), passed)
                    if a:
                        sp.wait_ge(max_full, HALVES * (n + 1))
                    if type(n) is int and n < 0:
                        if par == 0:
                            sp.wait_ge(mask_ok, 1)
                        else:
                            sp.wait_ge(q_mask1_ok, 1)
                    for j in range(J):
                        rows = slice(j * ROWS, j * ROWS + SHIFT)
                        sp.dma_start(q_mask[par][rows, j, :].bitcast(F32),
                                     q_raw[par][rows, :].bitcast(F32)).then_inc(qmask_in[par], 16)

            def store(n, h):
                wait_apart(sp, res_ok, 2 * n + h + 1 + 2, passed)
                dst = out_v[:, bass.ds(n // HG, 1), bass.ds(n % HG, 1), h, :, :]
                sp.dma_start(dst.rearrange("p b g t f -> p (b g t) f"), result[h][:, :, :]).then_inc(res_st[h], 16)

            items(sp, body)
            for h in range(2):
                sp.wait_ge(res_st[h], 16 * (N + 1))

        @block.gpsimd
        def _(pool):
            pool.sem_inc(res_ok, 2)
            for i in range(2):
                pool.sem_inc(res_st[i], 16)
            for i in range(2):
                nc.gpsimd.memset(v_st[i][:, :, :, D:D + 1], 1.0).then_inc(v_pad_ok, 1)
                nc.gpsimd.memset(v_st[i][:, :, :, D + 1:ROWS], 0.0).then_inc(v_pad_ok, 1)
            pool.wait_ge(const_in, 64)
            pool.wait_ge(stage_ok, 4)

            def operands(f, par):
                if not (type(f) is int and f < 2):
                    wait_apart(pool, pre_ok, 2 * (f - 1), passed)
                nc.gpsimd.tensor_copy(x_cur[par][:, :], xnT[:, bass.ds((f // HG) * T, T)]).then_inc(cur_ok, 1)
                nc.gpsimd.tensor_copy(w_cur[par][:, :], w_all[:, bass.ds(f % HG, 1), :]
                                      .rearrange("p a n -> p (a n)")).then_inc(cur_ok, 1)

            def front(f, par, base):
                own = Chain(pool, pool_own, base, passed)
                pool.wait_ge(exp_f_ok, f + 1)
                wait_apart(pool, pre_ok, 2 * (f + 1), passed)
                qk = pre[:, :, 0:2 * GF]
                flat = feat[:, :, :, :].rearrange("p t j d -> p t (j d)")
                own.did(nc.gpsimd.tensor_scalar(flat, qk, 0.0, None, ALU.max))
                own.did(nc.gpsimd.tensor_scalar(expd[:, :, :], expd[:, :, :], 1.0, None, ALU.min))
                nc.gpsimd.tensor_copy(v_raw[par][:, :, :, :].rearrange("p t j d -> p t (j d)"),
                                      pre[:, :, 2 * GF:W]).then_inc(front_ok, 1)
                own.settle()
                own.did(nc.gpsimd.tensor_tensor(flat, flat, expd[:, :, :], ALU.add))
                own.settle()
                cos_w = cosine[:, :, :].rearrange("p t (a d) -> p t a d", a=1).broadcast_to([P, KT, 2 * J, D // 2])
                sin_w = sine[:, :, :].rearrange("p t (a d) -> p t a d", a=1).broadcast_to([P, KT, 2 * J, D // 2])
                even, odd = feat[:, :, :, 0:D:2], feat[:, :, :, 1:D:2]
                for dst, src, table in ((0, even, cos_w), (1, odd, sin_w), (2, even, sin_w), (3, odd, cos_w)):
                    own.did(nc.gpsimd.tensor_tensor(rope[dst][:, :, :, :], src, table, ALU.mult))
                own.settle()
                own.did(nc.gpsimd.tensor_tensor(turned[:, :, :, 0:D:2], rope[0][:, :, :, :], rope[1][:, :, :, :],
                                                ALU.subtract))
                own.did(nc.gpsimd.tensor_tensor(turned[:, :, :, 1:D:2], rope[2][:, :, :, :], rope[3][:, :, :, :],
                                                ALU.add))
                own.settle(apart=True)
                if not (type(f) is int and f < 2):
                    wait_apart(pool, q_sh_ok, 2 * (f - 1), passed)
                st = stage[par]
                own.did(nc.gpsimd.tensor_copy(st[:, :, :, HI0:D].rearrange("p t j d -> p (t j) d"),
                                              turned[:, :, :, :].rearrange("p t j d -> p (t j) d")))
                own.did(nc.gpsimd.tensor_copy(st[:, :, 0:J, THIRD:THIRD + D], turned[:, :, 0:J, :]))
                own.did(nc.gpsimd.tensor_copy(st[:, :, J:2 * J, SECOND:SECOND + D], turned[:, :, J:2 * J, :]))
                own.settle()
                nc.gpsimd.tensor_tensor(st[:, :, 0:J, SECOND:SECOND + D], turned[:, :, 0:J, :],
                                        st[:, :, 0:J, HI0:D].bitcast(F32), ALU.subtract).then_inc(front_ok, 1)
                nc.gpsimd.tensor_tensor(st[:, :, J:2 * J, THIRD:THIRD + D], turned[:, :, J:2 * J, :],
                                        st[:, :, J:2 * J, HI0:D].bitcast(F32), ALU.subtract).then_inc(front_ok, 1)
                assert own.n == POOL_FRONT

            def shift(m, par, h, base):
                own = Chain(pool, pool_own, base, passed)
                wait_apart(pool, neg_ok, 2 * m + h + 1, passed)
                ts = slice(h * CT, (h + 1) * CT)
                src = neg_max[:, ts, :, :]
                hi = stage[par][:, ts, 0:J, SHIFT:SHIFT + 1]
                own.did(nc.gpsimd.tensor_copy(hi, src))
                own.settle()
                own.did(nc.gpsimd.tensor_tensor(stage[par][:, ts, 0:J, SHIFT + 1:SHIFT + 2], src,
                                                hi.bitcast(F32), ALU.subtract))
                own.settle()
                pool.sem_inc(shift_ok, 1)
                assert own.n == POOL_MAX

            def values(m, par):
                if not (type(m) is int and m < 2):
                    pool.wait_ge(pv_ok, GROUPS * (m - 1) + 2)
                wait_apart(pool, front_ok, 3 * m + 1, passed)
                nc.gpsimd.tensor_copy(v_st[par][:, :, :, 0:D].rearrange("p t j d -> p (t j) d"),
                                      v_raw[par][:, :, :, :].rearrange("p t j d -> p (t j) d")).then_inc(v_st_ok, 1)

            def combine(n, par, h, base):
                own = Chain(pool, pool_own, base, passed)
                pool.wait_ge(attn_ok, 2 * n + h + 1)
                pool.wait_ge(rest_in[par], 16 * (n // 2 + 1))
                if not (type(n) is int and n == 0):
                    pool.wait_ge(res_st[h], 16 * (n + 1))
                a_v = attn[h][:, :, :, :].rearrange("p t j d -> p t (j d)")
                gate = silu_t[:, bass.ds((n // HG) * KT + h * CT, CT), bass.ds((n % HG) * GF, GF)]
                own.did(nc.gpsimd.tensor_tensor(result[h][:, :, :], a_v, gate, ALU.mult))
                own.settle()
                nc.gpsimd.tensor_tensor(result[h][:, :, :], result[h][:, :, :],
                                        rest[par][:, h * CT:(h + 1) * CT, :], ALU.add).then_inc(res_ok, 1)

            def steps_of(n):
                a, m, f = has(n)
                return POOL_OUT * (after(n) + a) + POOL_MAX * (a + m) + POOL_FRONT * f

            def steps_before(n):
                if type(n) is int and n < 1:
                    return sum(steps_of(i) for i in range(-2, n))
                if type(n) is not int or n <= N - 2:
                    return steps_before(0) + POOL_STEPS * n - POOL_OUT
                return steps_before(n - 1) + steps_of(n - 1)

            def body(n, par):
                a, m, f = has(n)
                base = steps_before(n)
                if f:
                    operands(n + 2, par)
                if type(n) is int and n == -1:
                    nc.gpsimd.memset(q_mask[1][:, :, :].bitcast(F32), 0.0).then_inc(q_mask1_ok, 1)
                if after(n):
                    combine(n - 1, 1 - par, 1, base)
                    base = base + POOL_OUT
                if a:
                    shift(n, par, 1, base)
                    base = base + POOL_MAX
                if f:
                    front(n + 2, par, base)
                    base = base + POOL_FRONT
                if m:
                    values(n + 1, 1 - par)
                if a:
                    combine(n, par, 0, base)
                    base = base + POOL_OUT
                if m:
                    shift(n + 1, 1 - par, 0, base)
                    base = base + POOL_MAX

            items(pool, body)

        @block.tensor
        def _(pe):
            pe.wait_ge(stage_ok, 4)
            pe.wait_ge(v_pad_ok, 4)
            pe.sem_inc(pv_ok, 2)

            def score(n, par, s):
                qh, kt, j = s // (KT * J), s // J % KT, s % J
                if s == 0:
                    pe.wait_ge(kmask_in[par], 16 * J * (n // 2 + 1))
                if s in (0, SLOTS // 2):
                    pe.wait_ge(q_sh_ok, 2 * n + qh + 1)
                pe.wait_ge(exp_ok, SLOTS * n + (s + 1 if s else SB))
                nc.tensor.matmul(s_ps[s % SB][:, :], k_mask[par][:, j, kt * P:(kt + 1) * P],
                                 q_sh[par][:, qh * CH:(qh + 1) * CH], start=True, stop=True).then_inc(s_full, 1)

            def weigh(n, par, g):
                kt = g % KT
                if g == 0:
                    pe.wait_ge(v_st_ok, n + 1)
                if kt == 0:
                    pe.wait_ge(pv_out, QH * n + g // KT + 1)
                pe.wait_ge(exp_ok, SLOTS * n + J * (g + 1) + SB)
                for j in range(J):
                    last = nc.tensor.matmul(pv_ps[j * ROWS:(j + 1) * ROWS, :], v_st[par][:, kt, j, :],
                                            prob[g % 2][:, j, :], start=kt == 0, stop=kt == KT - 1)
                last.then_inc(pv_ok, 1)

            def maxima(m, par, k):
                qt, j, kh = k // 2 // J, k // 2 % J, k % 2
                if k == 0:
                    pe.wait_ge(qmask_in[par], 16 * J * (m // 2 + 1))
                    pe.wait_ge(raw_ok, 4 * (m + 1))
                pe.wait_ge(max_ok, HALVES * (m + 1) + (k + 1 if k else MB))
                nc.tensor.matmul(m_ps[k % MB][:, :], q_mask[par][:, j, qt * P:(qt + 1) * P],
                                 k_raw[par][:, kh * CH:(kh + 1) * CH], start=True, stop=True).then_inc(max_full, 1)

            def rounds(n, par, slot):
                for kind, part, r in at(n, slot):
                    if kind == "qkv":
                        pe.wait_ge(cur_ok, 2 * (n + 3))
                    if kind in "kq":
                        pe.wait_ge(front_ok, 3 * (n + 3))
                    if kind == "shift":
                        pe.wait_ge(shift_ok, 2 * (n + (part == 0)) + part + 1)
                    if kind == "out":
                        pe.wait_ge(pv_out, QH * (n - part) + part + 1 + 1)
                    pe.wait_ge(round_free, r + 1)
                    for t in range(CT):
                        tile = part * CT + t
                        if kind == "qkv":
                            last = nc.tensor.matmul(bank[:, t * W:(t + 1) * W], x_cur[par][:, tile * P:(tile + 1) * P],
                                                    w_cur[par][:, :], start=True, stop=True)
                            continue
                        if kind == "out":
                            src = pv_sb[:, t * P:(t + 1) * P]
                        else:
                            st = stage[par if kind != "shift" or part == 1 else 1 - par]
                            heads = slice(J, 2 * J) if kind == "k" else slice(0, J)
                            src = st[:, tile, heads, :].rearrange("p j r -> p (j r)").bitcast(F32)
                        last = nc.tensor.transpose(bank[:, t * P:(t + 1) * P], src, ident[:, :])
                    last.then_inc(round_full, 1)

            def body(n, par):
                a, m, f = has(n)
                for s in range(SLOTS):
                    if a:
                        score(n, par, s)
                    if m:
                        maxima(n + 1, 1 - par, s)
                    if a and s % J == 2 and s > J:
                        weigh(n, par, s // J - 1)
                    if s == 2 and after(n):
                        weigh(n - 1, 1 - par, GROUPS - 1)
                    rounds(n, par, s)

            items(pe, body)

        @block.scalar
        def _(act):
            act.sem_inc(exp_ok, SB)

            def soften(n, par, s):
                qh, kt, j = s // (KT * J), s // J % KT, s % J
                if j == 0:
                    act.wait_ge(pv_ok, GROUPS * n + s // J + 1)
                act.wait_ge(s_full, SLOTS * n + s + 1)
                nc.scalar.activation(prob[s // J % 2][:, j, :], s_ps[s % SB][:, :], ACT.Exp, scale=SCALE)\
                  .then_inc(exp_ok, 1)

            def rounds(n, par, slot):
                for kind, part, r in at(n, slot):
                    if kind == "qkv" and part == 1:
                        act.wait_ge(pre_ok, 2 * (n + 3))
                        nc.scalar.activation(expd[:, :, :], pre[:, :, 0:2 * GF], ACT.Exp).then_inc(exp_f_ok, 1)
                    if kind in ("k", "q", "shift"):
                        act.wait_ge(round_full, r + 1)
                        other = kind == "shift" and part == 0
                        dst = {"k": k_raw, "q": q_raw, "shift": q_sh}[kind][1 - par if other else par]
                        if kind == "k" and has(n)[0]:
                            act.wait_ge(max_full, HALVES * (n + 1))
                            act.wait_ge(kmask_in[par], 16 * J * (n // 2 + 1))
                        if kind == "q" and has(n)[0]:
                            act.wait_ge(qmask_in[par], 16 * J * (n // 2 + 1))
                        nc.scalar.activation(dst[:, part * CH:(part + 1) * CH], bank[:, :], ACT.Copy)\
                          .then_inc(q_sh_ok if kind == "shift" else raw_ok, 1)
                        done = (2 * (n + (part == 0)) + part + 1) if kind == "shift" \
                            else 4 * (n + 2) + 2 * (kind == "q") + part + 1
                        act.wait_ge(q_sh_ok if kind == "shift" else raw_ok, done)
                        act.sem_inc(round_free, 1)

            def body(n, par):
                a, m, f = has(n)
                for s in range(SLOTS):
                    if a:
                        soften(n, par, s)
                    rounds(n, par, s)

            items(act, body)

        @block.vector
        def _(dve):
            dve.sem_inc(max_ok, HALVES + MB)
            dve.sem_inc(round_free, 1)
            dve.sem_inc(pv_out, 1)
            for i in range(2):
                nc.vector.memset(stage[i][:, :, 0:J, SHIFT:ROWS].bitcast(F32), 0.0).then_inc(stage_ok, 1)
                nc.vector.memset(stage[i][:, :, J:2 * J, SHIFT:SHIFT + 2].bitcast(F32), 1.0)
                nc.vector.memset(stage[i][:, :, J:2 * J, SHIFT + 2:ROWS].bitcast(F32), 0.0).then_inc(stage_ok, 1)

            def largest(m, par, k):
                qt, j, kh = k // 2 // J, k // 2 % J, k % 2
                dve.wait_ge(max_full, HALVES * m + k + 1)
                nc.vector.tensor_reduce(out=neg_half[par][:, qt, j, kh:kh + 1], in_=m_ps[k % MB][:, :], axis=AX.X,
                                        op=ALU.max, negate=True)\
                   .then_inc(max_ok, 1)
                if (k + 1) % (HALVES // 2) == 0:
                    h = k // (HALVES // 2)
                    ts = slice(h * CT, (h + 1) * CT)
                    dve.wait_ge(max_ok, HALVES * (m + 1) + k + 1 + MB)
                    if not (type(m) is int and m == 0):
                        dve.wait_ge(shift_ok, 2 * (m - 1) + h + 1)
                    nc.vector.tensor_tensor(neg_max[:, ts, :, :], neg_half[par][:, ts, :, 0:1],
                                            neg_half[par][:, ts, :, 1:2], ALU.min).then_inc(neg_ok, 1)

            def rounds(n, par, slot):
                for kind, part, r in at(n, slot):
                    if kind == "qkv":
                        dve.wait_ge(round_full, r + 1)
                        f = n + 2
                        if part == 0 and not (type(n) is int and n < -1):
                            dve.wait_ge(front_ok, 3 * f)
                        wide = bias[:, bass.ds(f % HG, 1), :].broadcast_to([P, CT, W])
                        nc.vector.tensor_tensor(pre[:, part * CT:(part + 1) * CT, :],
                                                bank[:, 0:CT * W].rearrange("p (t w) -> p t w", w=W),
                                                wide, ALU.add).then_inc(pre_ok, 1)
                        dve.wait_ge(pre_ok, 2 * f + part + 1)
                        dve.sem_inc(round_free, 1)
                    if kind == "out":
                        dve.wait_ge(round_full, r + 1)
                        v = bank[:, :].rearrange("p (t j r) -> p t j r", t=CT, r=ROWS)
                        nc.vector.reciprocal(r_sum[:, :, :, :], v[:, :, :, D:D + 1]).then_inc(rsum_ok, 1)
                        item = n - part
                        dve.wait_ge(rsum_ok, 2 * item + part + 1)
                        dve.wait_ge(res_ok, 2 * (item - 1) + part + 1 + 2)
                        nc.vector.tensor_tensor(attn[part][:, :, :, :], v[:, :, :, 0:D],
                                                r_sum[:, :, :, :].broadcast_to([P, CT, J, D]),
                                                ALU.mult).then_inc(attn_ok, 1)
                        dve.wait_ge(attn_ok, 2 * item + part + 1)
                        dve.sem_inc(round_free, 1)

            def take_values(n, h):
                dve.wait_ge(pv_ok, GROUPS * n + (h + 1) * KT + 2)
                nc.vector.tensor_copy(pv_sb[:, :], pv_ps[:, :]).then_inc(pv_out, 1)

            def body(n, par):
                a, m, f = has(n)
                if type(n) is int and n == -1:
                    for mask in (q_mask[0], k_mask[0], k_mask[1]):
                        nc.vector.memset(mask[:, :, :].bitcast(F32), 0.0).then_inc(mask_ok, 1)
                for s in range(SLOTS):
                    if m:
                        largest(n + 1, 1 - par, s)
                    if a and s == SLOTS // 2 + 2:
                        take_values(n, 0)
                    if s == 3 and after(n):
                        take_values(n - 1, 1)
                    rounds(n, par, s)

            items(dve, body)


def build(nc, io):
    with ExitStack() as ctx:
        keep = {
            "ident": ctx.enter_context(nc.sbuf_tensor("ident", [P, P], F32)),
            "xnT": ctx.enter_context(nc.sbuf_tensor("xnT", [P, NTOK], F32)),
            "silu_t": ctx.enter_context(nc.sbuf_tensor("silu_t", [P, TILES, C], F32)),
        }
        io["gate_scratch"] = nc.dram_tensor("gate_scratch", [TILES * ER, P], F32).ap()
        io["rest_scratch"] = nc.dram_tensor("rest_scratch", [NTOK, C], F32).ap()
        with ExitStack() as c2:
            psum = [c2.enter_context(nc.psum_tensor(f"ps{i}", [P, 512], F32)) for i in range(8)]
            ffn = {k: c2.enter_context(nc.sbuf_tensor(k, [P, NTOK], F32R)) for k in ("xrh", "xrl")}
            ffn |= {k: c2.enter_context(nc.sbuf_tensor(k, [P, E, HID], F32R)) for k in ("w1h", "w1l", "w2h", "w2l")}
            small = {"b1": E * HT, "b2": E, "wv": C, "cols": 5}
            ffn |= {k: c2.enter_context(nc.sbuf_tensor(k, [P, n], F32)) for k, n in small.items()}
            prologue(nc, keep, ffn, io, psum)
            experts(nc, keep, ffn, io, psum)
        with ExitStack() as c3:
            psum = [c3.enter_context(nc.psum_tensor(f"pa{i}", [P, 512], F32)) for i in range(8)]
            attention(nc, keep, io, psum)


def kernel(**inputs):
    import numpy as np
    import concourse.bacc as bacc
    from concourse.bass_utils import run_bass_kernel_spmd

    a = {k[3:]: np.asarray(v) for k, v in inputs.items()}
    w = a["attn_w_qkv"].reshape(3, HG, GF, C)
    bq = a["attn_b_qkv"].reshape(3, HG, GF)

    def lay(x):
        return np.ascontiguousarray(x)

    w1 = np.concatenate([a["ffn_W1_s"], a["ffn_W1_r"]])
    w2 = np.concatenate([a["ffn_W2_s"], a["ffn_W2_r"]])
    b1 = np.concatenate([a["ffn_b1_s"], a["ffn_b1_r"]])
    b2 = np.concatenate([a["ffn_b2_s"], a["ffn_b2_r"]])
    pos = np.arange(T, dtype=np.float32)[:, None]
    div = np.exp(np.arange(0, D, 2, dtype=np.float32) * np.float32(-np.log(10000.0) / D)).astype(np.float32)
    ang = pos * div
    def table(f):
        return lay(f(ang).astype(np.float32).reshape(BT, P, D // 2).transpose(1, 0, 2))

    arrays = {
        "x": lay(a["attn_x"]),
        "ident": np.eye(P, dtype=np.float32),
        "rank": lay(np.broadcast_to(np.arange(ER, 0, -1, dtype=np.float32), (P, TILES, ER))),
        "cosine": table(np.cos),
        "sine": table(np.sin),
        "cent": lay(a["ffn_centroids"]),
        "gains": lay(np.stack([a["ffn_g_shared"]] * ES + [a["ffn_g_routed"]] * ER, axis=1)),
        "w1": lay(w1.transpose(1, 0, 2)),
        "w2": lay(w2.reshape(E, HT, P, C).transpose(2, 0, 1, 3).reshape(P, E, HID)),
        "b1": lay(b1.reshape(E * HT, P).T),
        "b2": lay(b2.T),
        "wv": lay(w[2].reshape(C, C).T),
        "cols": lay(np.concatenate([a["attn_w_lepe"][:, 0, :], a["attn_b_lepe"][:, None],
                                    a["attn_b_qkv"][2 * C:, None]], axis=1)),
        "wqkv": lay(w.transpose(3, 1, 0, 2).reshape(C, HG, 3 * GF)),
        "bqkv": lay(np.broadcast_to(bq.transpose(1, 0, 2).reshape(1, HG, 3 * GF), (P, HG, 3 * GF))),
    }
    nc = bacc.Bacc("TRN2", target_bir_lowering=False, num_devices=1)
    io = {k: nc.dram_tensor(f"in_{k}", v.shape, mybir.dt.from_np(v.dtype), kind="ExternalInput").ap()
          for k, v in arrays.items()}
    io["out"] = nc.dram_tensor("out", (B, T, C), F32, kind="ExternalOutput").ap()
    build(nc, io)
    r = run_bass_kernel_spmd(nc, [{f"in_{k}": v for k, v in arrays.items()}], core_ids=[0])
    return r.results[0]["out"]
```

```python
import concourse.bass as bass
from concourse import mybir
from contextlib import ExitStack

P = 128
C = 128
B, T = 4, 1024
NTOK = B * T
TILES = NTOK // P
BT = T // P
H, D = 16, 8
HG, J = 4, 4
GF = J * D
HID = 512
HT = HID // P
ES, ER = 2, 8
E = ES + ER
CH = 512
NCH = NTOK // CH
CT = CH // P
SCALE = float(D) ** -0.5
LN_EPS = 1e-5
RMS_EPS = 1.1920929e-07

F32 = mybir.dt.float32
F32R = mybir.dt.float32r
ALU = mybir.AluOpType
ACT = mybir.ActivationFunctionType
AX = mybir.AxisListType


def wait_apart(eng, sem, value, passed):
    eng.wait_ge(sem, value)
    eng.sem_inc(passed, 1)


class Chain:

    def __init__(self, eng, sem, base=0, passed=None):
        self.eng, self.sem, self.base, self.n, self.passed = eng, sem, base, 0, passed

    def did(self, ins):
        ins.then_inc(self.sem, 1)
        self.n += 1
        return ins

    def settle(self, apart=False):
        self.eng.wait_ge(self.sem, self.base + self.n)
        if apart:
            self.eng.sem_inc(self.passed, 1)


def prologue(nc, keep, ffn, io, psum):
    QT = BT
    EH = E // 2
    STEPS = 6
    with ExitStack() as ctx:
        def sb(name, shape, dt=F32):
            return ctx.enter_context(nc.sbuf_tensor(name, shape, dt))

        def sem(name):
            return ctx.enter_context(nc.semaphore(name))

        x_q = sb("x_q", [P, B, QT, C])
        xn_q = [sb(f"xn_q{i}", [P, QT, C]) for i in range(2)]
        xr_q = [sb(f"xr_q{i}", [P, QT, C]) for i in range(2)]
        w1_in = sb("w1_in", [P, EH, HID])
        w2_in = sb("w2_in", [P, EH, HID])
        gains = sb("gains", [P, E])
        cent = sb("cent", [P, ER])
        rank = sb("rank", [P, TILES, ER])
        st = sb("st", [P, QT, 6])
        mv = sb("mv", [P, QT, 2])
        var_eps = sb("var_eps", [P, QT])
        sd = sb("sd", [P, QT])
        rstd = sb("rstd", [P, QT])
        rvar = sb("rvar", [P, QT])
        ms = sb("ms", [P, QT])
        ms_eps = sb("ms_eps", [P, QT])
        rms = sb("rms", [P, QT])
        rrms = sb("rrms", [P, QT])
        th = sb("th", [P, TILES, ER])
        score = sb("score", [P, TILES, ER])
        left = sb("left", [P, TILES, ER])
        hit = sb("hit", [P, TILES, ER])
        pick = [sb(f"pick{i}", [P, TILES, ER]) for i in range(2)]
        best = sb("best", [P, TILES])
        total = sb("total", [P, TILES])
        rtotal = sb("rtotal", [P, TILES])
        gate = sb("gate", [P, TILES, ER])
        gateT = sb("gateT", [P, 2, P])

        tr_n = [psum[0], psum[1]]
        tr_r = [psum[2], psum[3]]
        logit = psum[4]
        tr_g = psum[5]

        const_in = sem("p_const_in")
        ffn_in = sem("p_ffn_in")
        passed = sem("p_passed")
        x_in = [sem(f"p_x_in{i}") for i in range(2)]
        w1_ld = sem("p_w1_in")
        w2_ld = sem("p_w2_in")
        w1_used = sem("p_w1_used")
        w2_used = sem("p_w2_used")
        w2_hi = sem("p_w2_hi")
        w1_hi = sem("p_w1_hi")
        own = sem("p_own")
        route = sem("p_route")
        var_ok = sem("p_var_ok")
        sd_ok = sem("p_sd_ok")
        xn_ok = sem("p_xn_ok")
        ms_ok = sem("p_ms_ok")
        rms_ok = sem("p_rms_ok")
        rrms_ok = sem("p_rrms_ok")
        xr_ok = sem("p_xr_ok")
        xr_hi = sem("p_xr_hi")
        xnT_full = sem("p_xnT_full")
        xnT_out = sem("p_xnT_out")
        xrT_full = sem("p_xrT_full")
        xrT_out = sem("p_xrT_out")
        logit_ok = sem("p_logit_ok")
        th_ok = sem("p_th_ok")
        gate_ok = sem("p_gate_ok")
        gateT_full = sem("p_gateT_full")
        gateT_ok = sem("p_gateT_ok")
        gateT_st = sem("p_gateT_st")

        ident = keep["ident"]
        xnT = keep["xnT"]
        block = ctx.enter_context(nc.Block())

        @block.sync
        def _(sp):
            x_v = io["x"].rearrange("b (t p) c -> b p t c", p=P)
            for i in range(2):
                sp.dma_start(x_q[:, i, :, :], x_v[i, :, :, :]).then_inc(x_in[i], 16)
                if i == 0:
                    sp.dma_start(ident[:, :], io["ident"]).then_inc(const_in, 16)
                    sp.dma_start(gains[:, :], io["gains"]).then_inc(const_in, 16)
                    sp.dma_start(cent[:, :], io["cent"]).then_inc(const_in, 16)
                    sp.dma_start(rank[:, :, :], io["rank"]).then_inc(const_in, 16)
                    sp.dma_start(w2_in[:, :, :], io["w2"][:, 0:EH, :]).then_inc(w2_ld, 16)
            sp.dma_start(w1_in[:, :, :], io["w1"][:, 0:EH, :]).then_inc(w1_ld, 16)
            for i in range(2):
                sp.wait_ge(x_in[i], 16)
                sp.dma_start(x_q[:, 2 + i, :, :], x_v[2 + i, :, :, :]).then_inc(x_in[i], 16)
            for k in ("b1", "b2", "wv", "cols"):
                sp.dma_start(ffn[k][:, :], io[k]).then_inc(ffn_in, 16)
            sp.wait_ge(w2_used, EH)
            sp.dma_start(w2_in[:, :, :], io["w2"][:, EH:E, :]).then_inc(w2_ld, 16)
            sp.wait_ge(w1_used, EH)
            sp.dma_start(w1_in[:, :, :], io["w1"][:, EH:E, :]).then_inc(w1_ld, 16)
            sp.wait_ge(gateT_ok, 1)
            for h in range(2):
                sp.dma_start(io["gate_scratch"][h * P:(h + 1) * P, :], gateT[:, h, :]).then_inc(gateT_st, 16)
            sp.wait_ge(gateT_st, 32)
            sp.wait_ge(ffn_in, 64)

        @block.gpsimd
        def _(pool):
            for h in range(2):
                pool.wait_ge(w2_ld, 16 * (h + 1))
                with pool.Fori(0, EH) as k:
                    whole = w2_in[:, bass.ds(k, 1), :].rearrange("p a n -> p (a n)")
                    hi, lo = (m[:, bass.ds(k + h * EH, 1), :].rearrange("p a n -> p (a n)")
                              for m in (ffn["w2h"], ffn["w2l"]))
                    nc.gpsimd.tensor_copy(hi, whole).then_inc(w2_hi, 1)
                    pool.wait_ge(w2_hi, k + h * EH + 1)
                    nc.gpsimd.tensor_tensor(lo, whole, hi.bitcast(F32), ALU.subtract).then_inc(w2_used, 1)

        @block.vector
        def _(dve):
            dve.sem_inc(xrT_out, 2)

            def batch(b, i, pair):
                own_steps = Chain(dve, own, b * STEPS, passed)
                xb = x_q[:, bass.ds(b, 1), :, :].rearrange("p a t c -> p (a t) c")
                dve.wait_ge(x_in[i], 16 * (pair + 1))
                for t in range(QT):
                    last = nc.vector.bn_stats(st[:, t, :], xb[:, t, :])
                own_steps.did(last)
                if not (type(b) is int and b == 0):
                    low_parts(b - 1)
                own_steps.settle(apart=True)
                for t in range(QT):
                    last = nc.vector.bn_aggr(mv[:, t, :], st[:, t, :])
                own_steps.did(last)
                own_steps.settle()
                nc.vector.tensor_scalar(var_eps[:, :], mv[:, :, 1], LN_EPS, None, ALU.add).then_inc(var_ok, 1)
                dve.wait_ge(var_ok, b + 1)
                own_steps.did(nc.vector.reciprocal(rvar[:, :], var_eps[:, :]))
                own_steps.settle()
                own_steps.did(nc.vector.tensor_tensor(ms[:, :], mv[:, :, 1], rvar[:, :], ALU.mult))
                own_steps.settle()
                nc.vector.tensor_scalar(ms_eps[:, :], ms[:, :], RMS_EPS, None, ALU.add).then_inc(ms_ok, 1)
                dve.wait_ge(sd_ok, b + 1)
                own_steps.did(nc.vector.reciprocal(rstd[:, :], sd[:, :]))
                dve.wait_ge(rms_ok, b + 1)
                own_steps.did(nc.vector.reciprocal(rrms[:, :], rms[:, :]))
                own_steps.settle()
                dve.sem_inc(rrms_ok, 1)
                dve.wait_ge(xnT_full, 2 * b + 2)
                for t in range(QT):
                    nc.vector.tensor_scalar(xn_q[i][:, t, :], xb[:, t, :], mv[:, t, 0:1], rstd[:, t:t + 1],
                                            ALU.subtract, ALU.mult).then_inc(xn_ok, 1)
                assert own_steps.n == STEPS

            def low_parts(b):
                for h in range(2):
                    cols = bass.ds(b * T + h * CH, CH)
                    dve.wait_ge(xr_hi, 2 * b + h + 1)
                    nc.vector.tensor_tensor(ffn["xrl"][:, cols], tr_r[h][:, :],
                                            ffn["xrh"][:, cols].bitcast(F32), ALU.subtract).then_inc(xrT_out, 1)

            def first_lows(first, last):
                for e in range(first, last):
                    k = e % EH
                    dve.wait_ge(w1_hi, e + 1)
                    nc.vector.scalar_tensor_tensor(ffn["w1l"][:, e, :], w1_in[:, k, :], gains[:, e:e + 1],
                                                   ffn["w1h"][:, e, :].bitcast(F32),
                                                   ALU.mult, ALU.subtract).then_inc(w1_used, 1)

            batch(0, 0, 0)
            batch(1, 1, 0)
            batch(2, 0, 1)
            first_lows(0, 3)
            batch(3, 1, 1)
            low_parts(3)
            first_lows(3, EH)

            def wide(m):
                return m.rearrange("p (t a) -> p t a", a=1).broadcast_to([P, TILES, ER])

            r = Chain(dve, route)
            dve.wait_ge(th_ok, 1)
            r.did(nc.vector.tensor_scalar(score[:, :, :], th[:, :, :], 0.5, 0.5, ALU.mult, ALU.add))
            r.settle()
            r.did(nc.vector.reduce_sum(total[:, :], score[:, :, :], axis=AX.X))
            r.settle()
            r.did(nc.vector.reciprocal(rtotal[:, :], total[:, :]))
            for k in range(2):
                src = score if k == 0 else left
                r.did(nc.vector.reduce_max(best[:, :], src[:, :, :], axis=AX.X))
                r.settle()
                r.did(nc.vector.tensor_tensor(hit[:, :, :], src[:, :, :], wide(best[:, :]), ALU.is_ge))
                r.settle()
                r.did(nc.vector.tensor_tensor(hit[:, :, :], hit[:, :, :], rank[:, :, :], ALU.mult))
                r.settle()
                r.did(nc.vector.reduce_max(best[:, :], hit[:, :, :], axis=AX.X))
                r.settle()
                r.did(nc.vector.tensor_tensor(pick[k][:, :, :], hit[:, :, :], wide(best[:, :]), ALU.is_equal))
                r.settle()
                if k == 0:
                    r.did(nc.vector.scalar_tensor_tensor(left[:, :, :], pick[0][:, :, :], -4.0, score[:, :, :],
                                                         ALU.mult, ALU.add))
                    r.settle()
            r.did(nc.vector.tensor_tensor(pick[0][:, :, :], pick[0][:, :, :], pick[1][:, :, :], ALU.add))
            r.settle()
            r.did(nc.vector.tensor_tensor(gate[:, :, :], pick[0][:, :, :], score[:, :, :], ALU.mult))
            r.settle()
            nc.vector.tensor_tensor(gate[:, :, :], gate[:, :, :], wide(rtotal[:, :]), ALU.mult).then_inc(gate_ok, 1)
            first_lows(EH, EH + 1)
            dve.wait_ge(gateT_full, 2)
            nc.vector.tensor_copy(gateT[:, :, :].rearrange("p h n -> p (h n)"), tr_g[:, 0:2 * P]).then_inc(gateT_ok, 1)
            first_lows(EH + 1, E)

        @block.scalar
        def _(act):
            act.sem_inc(xnT_out, 2)

            def first_matrix(k, h):
                e = h * EH + k
                nc.scalar.activation(ffn["w1h"][:, bass.ds(e, 1), :].rearrange("p a n -> p (a n)"), w1_in[:, k, :],
                                     ACT.Copy, scale=gains[:, bass.ds(e, 1)]).then_inc(w1_hi, 1)

            for b in range(B):
                i = b % 2
                act.wait_ge(var_ok, b + 1)
                nc.scalar.activation(sd[:, :], var_eps[:, :], ACT.Sqrt).then_inc(sd_ok, 1)
                act.wait_ge(ms_ok, b + 1)
                nc.scalar.activation(rms[:, :], ms_eps[:, :], ACT.Sqrt).then_inc(rms_ok, 1)
                act.wait_ge(rrms_ok, b + 1)
                for t in range(QT):
                    act.wait_ge(xn_ok, QT * b + t + 1)
                    nc.scalar.activation(xr_q[i][:, t, :], xn_q[i][:, t, :], ACT.Copy,
                                         scale=rrms[:, t:t + 1]).then_inc(xr_ok, 1)
                for h in range(2):
                    act.wait_ge(xnT_full, 2 * b + h + 1 + 4)
                    nc.scalar.activation(xnT[:, b * T + h * CH:b * T + (h + 1) * CH], tr_n[h][:, :],
                                         ACT.Copy).then_inc(xnT_out, 1)
                for h in range(2):
                    act.wait_ge(xrT_full, 2 * b + h + 1)
                    nc.scalar.activation(ffn["xrh"][:, b * T + h * CH:b * T + (h + 1) * CH], tr_r[h][:, :],
                                         ACT.Copy).then_inc(xr_hi, 1)
                for k in ((), (0, 1, 2), (3, 4), ())[b]:
                    act.wait_ge(w1_ld, 16)
                    act.wait_ge(const_in, 64)
                    first_matrix(k, 0)
            act.wait_ge(logit_ok, 1)
            nc.scalar.activation(th[:, :, :], logit[:, 0:TILES * ER].rearrange("p (t e) -> p t e", e=ER),
                                 ACT.Tanh, scale=0.5).then_inc(th_ok, 1)
            act.wait_ge(w1_ld, 32)
            for k in range(EH):
                first_matrix(k, 1)

        @block.tensor
        def _(pe):
            pe.wait_ge(const_in, 64)
            pe.sem_inc(xnT_full, 4)
            for b in range(B):
                i = b % 2
                for h in range(2):
                    pe.wait_ge(xn_ok, QT * b + 4 * (h + 1))
                    pe.wait_ge(xnT_out, 2 * b + 2)
                    for k in range(4):
                        last = nc.tensor.transpose(tr_n[h][:, k * P:(k + 1) * P], xn_q[i][:, 4 * h + k, :],
                                                   ident[:, :])
                    last.then_inc(xnT_full, 1)
                for h in range(2):
                    pe.wait_ge(xr_ok, QT * b + 4 * (h + 1))
                    pe.wait_ge(xrT_out, 2 * b + 2)
                    for k in range(4):
                        last = nc.tensor.transpose(tr_r[h][:, k * P:(k + 1) * P], xr_q[i][:, 4 * h + k, :],
                                                   ident[:, :])
                    last.then_inc(xrT_full, 1)
                pe.wait_ge(xnT_out, 2 * b + 4)
                for t in range(b * BT, (b + 1) * BT):
                    last = nc.tensor.matmul(logit[:, t * ER:(t + 1) * ER], xnT[:, t * P:(t + 1) * P], cent[:, :],
                                            start=True, stop=True)
            last.then_inc(logit_ok, 1)
            pe.wait_ge(gate_ok, 1)
            flat = gate[:, :, :].rearrange("p t e -> p (t e)")
            for h in range(2):
                nc.tensor.transpose(tr_g[:, h * P:(h + 1) * P], flat[:, h * P:(h + 1) * P],
                                    ident[:, :]).then_inc(gateT_full, 1)


def experts(nc, keep, ffn, io, psum):
    NQ = E * HT
    NY = 1 + ER
    LAG = 3
    HB = 4
    TAIL_AT, CONV_AT = 10, 18
    TAPS_AT = (22, 25, 29)
    with ExitStack() as ctx:
        def sb(name, shape, dt=F32):
            return ctx.enter_context(nc.sbuf_tensor(name, shape, dt))

        def sem(name):
            return ctx.enter_context(nc.semaphore(name))

        hidden = [sb(f"hidden{i}", [P, CH]) for i in range(2)]
        hid_hi = [sb(f"hid_hi{i}", [P, CH], F32R) for i in range(HB)]
        hid_lo = [sb(f"hid_lo{i}", [P, CH], F32R) for i in range(HB)]
        gates = [sb(f"gates{i}", [P, CH]) for i in range(2)]
        gated = [sb(f"gated{i}", [P, CH]) for i in range(2)]
        acc = [sb(f"acc{i}", [P, CH]) for i in range(2)]
        tanh_g = sb("tanh_g", [P, CH])
        silu_g = sb("silu_g", [P, CH])
        lepe_g = sb("lepe_g", [P, CH])
        x_c = sb("x_c", [P, CT, C])
        rest = sb("rest", [P, CT, C])
        v_pad = sb("v_pad", [P, T + 2])
        lepe = sb("lepe", [P, T])
        b2s = sb("b2s", [P, 1])

        hid_ps = psum[0:HB]
        y_ps = psum[4:6]
        aux = [psum[6], psum[7]]

        passed = sem("f_passed")
        ready = sem("f_ready")
        hid_full = sem("f_hid_full")
        gelu_ok = sem("f_gelu_ok")
        hi_ok = sem("f_hi_ok")
        split_ok = sem("f_split_ok")
        down_ok = sem("f_down_ok")
        y_out = sem("f_y_out")
        gates_in = [sem(f"f_gates_in{i}") for i in range(2)]
        acc_ok = sem("f_acc_ok")
        tanh_ok = sem("f_tanh_ok")
        pool_own = sem("f_pool_own")
        tail_ok = sem("f_tail_ok")
        aux_full = sem("f_aux_full")
        silu_out = sem("f_silu_out")
        rest_ok = sem("f_rest_ok")
        x_c_in = sem("f_x_c_in")
        rest_st = sem("f_rest_st")
        v_full = sem("f_v_full")
        v_ok = sem("f_v_ok")
        conv_own = sem("f_conv_own")
        conv_ok = sem("f_conv_ok")

        ident, xnT, silu_t = keep["ident"], keep["xnT"], keep["silu_t"]
        b1, b2, wv, cols = (ffn[k] for k in ("b1", "b2", "wv", "cols"))
        block = ctx.enter_context(nc.Block())

        def chunks(eng, body):
            body(0, 0, False)
            with eng.Fori(0, (NCH - 2) // 2) as pair:
                body(pair * 2 + 1, 1, True)
                body(pair * 2 + 2, 0, True)
            body(NCH - 1, 1, True)

        def gate_slot(y):
            return (y - 1) % 2

        @block.sync
        def _(sp):
            gate_v = io["gate_scratch"].rearrange("(c t e) n -> c e t n", t=CT, e=ER)
            x_v = io["x"].rearrange("b (h t p) c -> (b h) p t c", p=P, t=CT)
            rest_v = io["rest_scratch"].rearrange("(c t p) n -> c p t n", p=P, t=CT)

            def load_x(c):
                sp.dma_start(x_c[:, :, :], x_v[bass.ds(c, 1), :, :, :].rearrange("a p t c -> p (a t) c"))\
                  .then_inc(x_c_in, 16)

            def store_rest(c):
                wait_apart(sp, rest_ok, c + 1, passed)
                sp.dma_start(rest_v[bass.ds(c, 1), :, :, :].rearrange("a p t c -> p (a t) c"), rest[:, :, :])\
                  .then_inc(rest_st, 16)

            def body(c, par, tail):
                for y in range(1, NY):
                    wait_apart(sp, y_out, c * NY + (y if y <= 2 else y + 1), passed)
                    src = gate_v[bass.ds(c, 1), y - 1, :, :]
                    sp.dma_start(gates[gate_slot(y)][:, :].rearrange("p (t n) -> p t n", n=P),
                                 src.broadcast_to([P, CT, P])).then_inc(gates_in[gate_slot(y)], 16)
                    if y == 4 and tail:
                        store_rest(c - 1)
                        load_x(c)

            sp.sem_inc(rest_st, 16)
            load_x(0)
            chunks(sp, body)
            store_rest(NCH - 1)
            sp.wait_ge(rest_st, 16 * (NCH + 1))

        @block.tensor
        def _(pe):
            pe.sem_inc(down_ok, HB)
            pe.sem_inc(aux_full, 2)

            def up(c, q):
                e, ht = q // HT, q % HT
                toks = bass.ds(c * CH, CH)
                m = slice(ht * P, (ht + 1) * P)
                bank = hid_ps[q % HB]
                pe.wait_ge(gelu_ok, c * NQ + q + 1)
                nc.tensor.matmul(bank[:, :], ffn["w1h"][:, e, m], ffn["xrh"][:, toks], start=True, stop=False)
                nc.tensor.matmul(bank[:, :], ffn["w1h"][:, e, m], ffn["xrl"][:, toks], start=False, stop=False)
                nc.tensor.matmul(bank[:, :], ffn["w1l"][:, e, m], ffn["xrh"][:, toks], start=False, stop=True)\
                  .then_inc(hid_full, 1)

            def down(c, par, q):
                e, ht = q // HT, q % HT
                y = max(0, e - ES + 1)
                first, last = q in (0, *range(ES * HT, NQ, HT)), ht == HT - 1 and e >= ES - 1
                bank = y_ps[(par + y) % 2]
                m = slice(ht * P, (ht + 1) * P)
                if first:
                    pe.wait_ge(y_out, c * NY + y + 1)
                pe.wait_ge(split_ok, c * NQ + q + 1 + 2)
                nc.tensor.matmul(bank[:, :], ffn["w2h"][:, e, m], hid_hi[q % HB][:, :], start=first, stop=False)
                nc.tensor.matmul(bank[:, :], ffn["w2l"][:, e, m], hid_hi[q % HB][:, :], start=False, stop=False)
                nc.tensor.matmul(bank[:, :], ffn["w2h"][:, e, m], hid_lo[q % HB][:, :], start=False, stop=last)\
                  .then_inc(down_ok, 1)

            def tail_transposes(c):
                pe.wait_ge(tail_ok, c + 1)
                pe.wait_ge(v_ok, 2 * (c // 2) + 2)
                for bank, src in ((aux[0], silu_g), (aux[1], lepe_g)):
                    for t in range(CT):
                        last = nc.tensor.transpose(bank[:, t * P:(t + 1) * P], src[:, t * P:(t + 1) * P], ident[:, :])
                    last.then_inc(aux_full, 1)

            def v_product(b, after):
                pe.wait_ge(silu_out, after)
                pe.wait_ge(rest_ok, after)
                for h in range(2):
                    nc.tensor.matmul(aux[h][:, :], wv[:, :], xnT[:, bass.ds(b * T + h * CH, CH)],
                                     start=True, stop=True).then_inc(v_full, 1)

            def body(c, par, tail):
                for q in range(NQ + LAG):
                    if q < NQ:
                        up(c, q)
                    if q == TAIL_AT and tail:
                        tail_transposes(c - 1)
                    if q == CONV_AT and par == 0:
                        v_product(c // 2, c)
                    if q >= LAG:
                        down(c, par, q - LAG)

            chunks(pe, body)
            tail_transposes(NCH - 1)

        @block.scalar
        def _(act):
            act.sem_inc(gelu_ok, HB)

            def tanh_part(c, par):
                act.wait_ge(acc_ok, (c + 1) * ER)
                nc.scalar.activation(tanh_g[:, :], acc[par][:, :], ACT.Tanh, scale=0.5).then_inc(tanh_ok, 1)

            def silu_part(c):
                act.wait_ge(aux_full, 2 * c + 1 + 2)
                nc.scalar.activation(silu_t[:, bass.ds(c * CT, CT), :],
                                     aux[0][:, :].rearrange("p (t n) -> p t n", n=P), ACT.Copy).then_inc(silu_out, 1)

            def body(c, par, tail):
                for q in range(NQ):
                    act.wait_ge(hid_full, c * NQ + q + 1)
                    act.wait_ge(split_ok, c * NQ + q + 1)
                    nc.scalar.activation(hidden[q % 2][:, :], hid_ps[q % HB][:, :], ACT.Gelu,
                                         bias=b1[:, q:q + 1]).then_inc(gelu_ok, 1)
                    if q == 3 and tail:
                        tanh_part(c - 1, 1 - par)
                    if q == TAIL_AT + 1 and tail:
                        silu_part(c - 1)
                    if q == CONV_AT + 1 and par == 0:
                        for h in range(2):
                            act.wait_ge(v_full, c + h + 1)
                            act.wait_ge(conv_ok, c // 2 + 1)
                            nc.scalar.activation(v_pad[:, 1 + h * CH:1 + (h + 1) * CH], aux[h][:, :],
                                                 ACT.Identity, bias=cols[:, 4:5]).then_inc(v_ok, 1)

            chunks(act, body)
            tanh_part(NCH - 1, 1)
            silu_part(NCH - 1)

        @block.vector
        def _(dve):
            dve.sem_inc(split_ok, 2)
            dve.sem_inc(y_out, 2)
            dve.sem_inc(conv_ok, 1)
            nc.vector.memset(v_pad[:, 0:1], 0.0)
            nc.vector.memset(v_pad[:, T + 1:T + 2], 0.0).then_inc(ready, 1)
            nc.vector.tensor_tensor(b2s[:, :], b2[:, 0:1], b2[:, 1:2], ALU.add).then_inc(ready, 1)
            dve.wait_ge(ready, 2)

            def split(c, q):
                dve.wait_ge(gelu_ok, c * NQ + q + 1 + HB)
                dve.wait_ge(down_ok, c * NQ + q + 1)
                nc.vector.tensor_copy(hid_hi[q % HB][:, :], hidden[q % 2][:, :]).then_inc(hi_ok, 1)
                dve.wait_ge(hi_ok, c * NQ + q + 1)
                nc.vector.tensor_tensor(hid_lo[q % HB][:, :], hidden[q % 2][:, :], hid_hi[q % HB][:, :].bitcast(F32),
                                        ALU.subtract).then_inc(split_ok, 1)

            def output(c, par, y):
                dve.wait_ge(down_ok, c * NQ + (ES + y) * HT + HB)
                bank = y_ps[(par + y) % 2]
                if y == 0:
                    nc.vector.scalar_tensor_tensor(acc[par][:, :], bank[:, :], b2s[:, 0:1],
                                                   xnT[:, bass.ds(c * CH, CH)], ALU.add, ALU.add)\
                      .then_inc(y_out, 1)
                    return
                slot = gate_slot(y)
                dve.wait_ge(gates_in[slot], 16 * (ER // 2) * c + 16 * ((y - 1) // 2 + 1))
                if y > 2 or not (type(c) is int and c == 0):
                    dve.wait_ge(acc_ok, c * ER + y - 2)
                nc.vector.scalar_tensor_tensor(gated[slot][:, :], bank[:, :], b2[:, ES + y - 1:ES + y],
                                               gates[slot][:, :], ALU.add, ALU.mult).then_inc(y_out, 1)

            def rest_part(c):
                dve.wait_ge(aux_full, 2 * c + 2 + 2)
                dve.wait_ge(x_c_in, 16 * (c + 1))
                dve.wait_ge(rest_st, 16 * (c + 1))
                nc.vector.tensor_tensor(rest[:, :, :], aux[1][:, :].rearrange("p (t n) -> p t n", n=P),
                                        x_c[:, :, :], ALU.add).then_inc(rest_ok, 1)

            def convolve(b, tails, tap):
                if tap == 0:
                    dve.wait_ge(v_ok, 2 * b + 2)
                    dve.wait_ge(tail_ok, tails)
                    nc.vector.tensor_scalar(lepe[:, :], v_pad[:, 1:T + 1], cols[:, 1:2], cols[:, 3:4],
                                            ALU.mult, ALU.add).then_inc(conv_own, 1)
                if tap == 1:
                    dve.wait_ge(conv_own, 2 * b + 1)
                    nc.vector.scalar_tensor_tensor(lepe[:, :], v_pad[:, 0:T], cols[:, 0:1], lepe[:, :],
                                                   ALU.mult, ALU.add).then_inc(conv_own, 1)
                if tap == 2:
                    dve.wait_ge(conv_own, 2 * b + 2)
                    nc.vector.scalar_tensor_tensor(lepe[:, :], v_pad[:, 2:T + 2], cols[:, 2:3], lepe[:, :],
                                                   ALU.mult, ALU.add).then_inc(conv_ok, 1)

            def body(c, par, tail):
                for q in range(NQ):
                    split(c, q)
                    if q == TAIL_AT + 2 and tail:
                        rest_part(c - 1)
                    if q in TAPS_AT and par == 0:
                        convolve(c // 2, c, TAPS_AT.index(q))
                    e, ht = (q - LAG - 1) // HT, (q - LAG - 1) % HT
                    if q > LAG and ht == HT - 1 and e >= ES - 1:
                        output(c, par, e - ES + 1)
                output(c, par, NY - 1)

            chunks(dve, body)
            rest_part(NCH - 1)

        @block.gpsimd
        def _(pool):
            def add(c, par, y):
                pool.wait_ge(y_out, c * NY + y + 1 + 2)
                pool.wait_ge(acc_ok, c * ER + y - 1)
                nc.gpsimd.tensor_tensor(acc[par][:, :], acc[par][:, :], gated[gate_slot(y)][:, :],
                                        ALU.add).then_inc(acc_ok, 1)

            def tail_part(c, par):
                wait_apart(pool, tanh_ok, c + 1, passed)
                own = Chain(pool, pool_own, 2 * c)
                own.did(nc.gpsimd.tensor_scalar(tanh_g[:, :], tanh_g[:, :], 0.5, 0.5, ALU.mult, ALU.add))
                own.settle()
                pool.wait_ge(aux_full, 2 * c + 2)
                own.did(nc.gpsimd.tensor_tensor(silu_g[:, :], acc[par][:, :], tanh_g[:, :], ALU.mult))
                own.settle()
                pool.wait_ge(conv_ok, c // 2 + 2)
                nc.gpsimd.tensor_tensor(lepe_g[:, :], lepe[:, par * CH:(par + 1) * CH], silu_g[:, :],
                                        ALU.mult).then_inc(tail_ok, 1)

            def body(c, par, tail):
                if tail:
                    tail_part(c - 1, 1 - par)
                for y in range(1, NY):
                    add(c, par, y)

            chunks(pool, body)
            tail_part(NCH - 1, 1)


def attention(nc, keep, io, psum):
    N = B * HG
    KT = T // P
    QH = T // CH
    SLOTS = QH * KT * J
    GROUPS = QH * KT
    HALVES = 2 * KT * J
    SB, MB = 3, 3
    W = 3 * GF
    ROWS = 32
    HI0, SECOND, THIRD, SHIFT = 0, D, 2 * D, 3 * D
    ROUNDS = 10
    LEAD = 45
    FRONT_STEPS, POOL_OUT = 12, 1
    POOL_STEPS = FRONT_STEPS + QH * POOL_OUT
    AT_SHIFT1, AT_QKV, AT_K, AT_Q, AT_SHIFT0, AT_LAST_OUT = 23, (13, 17), (47, 51), (57, 61), 54, 7

    with ExitStack() as ctx:
        def sb(name, shape, dt=F32):
            return ctx.enter_context(nc.sbuf_tensor(name, shape, dt))

        def sem(name):
            return ctx.enter_context(nc.semaphore(name))

        x_cur = [sb(f"x_cur{i}", [P, T]) for i in range(2)]
        w_cur = [sb(f"w_cur{i}", [P, W]) for i in range(2)]
        w_all = sb("w_all", [P, HG, W])
        bias = sb("bias", [P, HG, W])
        cosine = sb("cosine", [P, KT, D // 2])
        sine = sb("sine", [P, KT, D // 2])
        pre = sb("pre", [P, KT, W])
        expd = sb("expd", [P, KT, 2 * GF])
        feat = sb("feat", [P, KT, 2 * J, D])
        rope = [sb(f"rope{i}", [P, KT, 2 * J, D // 2]) for i in range(4)]
        turned = sb("turned", [P, KT, 2 * J, D])
        ident_r = sb("ident_r", [P, P], F32R)
        stage = [sb(f"stage{i}", [P, KT, 2 * J, ROWS], F32R) for i in range(2)]
        v_raw = [sb(f"v_raw{i}", [P, KT, J, D]) for i in range(2)]
        v_st = [sb(f"v_st{i}", [P, KT, J, ROWS]) for i in range(2)]
        k_raw = [sb(f"k_raw{i}", [P, T], F32R) for i in range(2)]
        q_raw = [sb(f"q_raw{i}", [P, T], F32R) for i in range(2)]
        k_mask = [sb(f"k_mask{i}", [P, J, T], F32R) for i in range(2)]
        q_mask = [sb(f"q_mask{i}", [P, J, T], F32R) for i in range(2)]
        q_sh = [sb(f"q_sh{i}", [P, T], F32R) for i in range(2)]
        shift = [sb(f"shift{i}", [P, J, 2, CT], F32R) for i in range(2)]
        shift_t = [sb(f"shift_t{i}", [J * 2 * CT, P], F32R) for i in range(2)]
        neg_half = [sb(f"neg_half{i}", [P, KT, J, 2]) for i in range(2)]
        neg_max = sb("neg_max", [P, KT, J, 1])
        prob = [sb(f"prob{i}", [P, J, CH]) for i in range(2)]
        pv_sb = sb("pv_sb", [P, CH])
        r_sum = sb("r_sum", [P, CT, J, 1])
        attn = [sb(f"attn{i}", [P, CT, J, D]) for i in range(2)]
        rest = [sb(f"rest_a{i}", [P, KT, GF]) for i in range(2)]
        result = [sb(f"result{i}", [P, CT, GF]) for i in range(2)]

        s_ps = psum[0:SB]
        m_ps = psum[SB:SB + MB]
        pv_ps = psum[6]
        shared_ps = psum[7]

        w_in = sem("a_w_in")
        const_in = sem("a_const_in")
        passed = sem("a_passed")
        stage_ok = sem("a_stage_ok")
        v_pad_ok = sem("a_v_pad_ok")
        mask_ok = sem("a_mask_ok")
        dve_own = sem("a_dve_own")
        cur_ok = sem("a_cur_ok")
        round_full = sem("a_round_full")
        round_free = sem("a_round_free")
        pre_ok = sem("a_pre_ok")
        exp_f_ok = sem("a_exp_f_ok")
        pool_own = sem("a_pool_own")
        front_ok = sem("a_front_ok")
        raw_ok = sem("a_raw_ok")
        qmask_in = [sem(f"a_qmask_in{i}") for i in range(2)]
        kmask_in = [sem(f"a_kmask_in{i}") for i in range(2)]
        max_full = sem("a_max_full")
        max_ok = sem("a_max_ok")
        neg_ok = sem("a_neg_ok")
        shift_hi = sem("a_shift_hi")
        shift_ok = sem("a_shift_ok")
        shift_t_ok = sem("a_shift_t_ok")
        shift_in = [sem(f"a_shift_in{i}") for i in range(2)]
        q_sh_in = [sem(f"a_q_sh_in{i}") for i in range(2)]
        v_st_ok = sem("a_v_st_ok")
        s_full = sem("a_s_full")
        exp_ok = sem("a_exp_ok")
        pv_ok = sem("a_pv_ok")
        pv_out = sem("a_pv_out")
        rsum_ok = sem("a_rsum_ok")
        attn_ok = sem("a_attn_ok")
        res_ok = sem("a_res_ok")
        rest_in = [sem(f"a_rest_in{i}") for i in range(2)]
        res_st = [sem(f"a_res_st{i}") for i in range(2)]

        ident, xnT, silu_t = keep["ident"], keep["xnT"], keep["silu_t"]
        block = ctx.enter_context(nc.Block())

        def items(eng, body):
            for n in (-2, -1, 0):
                body(n, n % 2)
            with eng.Fori(0, (N - 4) // 2) as pair:
                body(pair * 2 + 1, 1)
                body(pair * 2 + 2, 0)
            for n in range(N - 3, N + 1):
                body(n, n % 2)

        def has(n):
            if type(n) is not int:
                return True, True, True
            return 0 <= n < N, 0 <= n + 1 < N, n + 2 < N

        def after(n):
            return type(n) is not int or 1 <= n <= N

        def operands(eng, api, f, par):
            if not (type(f) is int and f < 2):
                wait_apart(eng, pre_ok, 2 * (f - 1), passed)
            api.tensor_copy(x_cur[par][:, :], xnT[:, bass.ds((f // HG) * T, T)]).then_inc(cur_ok, 1)
            eng.wait_ge(w_in, 16)
            api.tensor_copy(w_cur[par][:, :], w_all[:, bass.ds(f % HG, 1), :]
                            .rearrange("p a n -> p (a n)")).then_inc(cur_ok, 1)

        def front(eng, api, f, par, own):
            eng.wait_ge(exp_f_ok, f + 1)
            wait_apart(eng, pre_ok, 2 * (f + 1), passed)
            qk = pre[:, :, 0:2 * GF]
            flat = feat[:, :, :, :].rearrange("p t j d -> p t (j d)")
            own.did(api.tensor_scalar(flat, qk, 0.0, None, ALU.max))
            own.did(api.tensor_scalar(expd[:, :, :], expd[:, :, :], 1.0, None, ALU.min))
            api.tensor_copy(v_raw[par][:, :, :, :].rearrange("p t j d -> p t (j d)"),
                            pre[:, :, 2 * GF:W]).then_inc(front_ok, 1)
            own.settle()
            own.did(api.tensor_tensor(flat, flat, expd[:, :, :], ALU.add))
            own.settle()
            cos_w = cosine[:, :, :].rearrange("p t (a d) -> p t a d", a=1).broadcast_to([P, KT, 2 * J, D // 2])
            sin_w = sine[:, :, :].rearrange("p t (a d) -> p t a d", a=1).broadcast_to([P, KT, 2 * J, D // 2])
            even, odd = feat[:, :, :, 0:D:2], feat[:, :, :, 1:D:2]
            for dst, src, table in ((0, even, cos_w), (1, odd, sin_w), (2, even, sin_w), (3, odd, cos_w)):
                own.did(api.tensor_tensor(rope[dst][:, :, :, :], src, table, ALU.mult))
            own.settle()
            own.did(api.tensor_tensor(turned[:, :, :, 0:D:2], rope[0][:, :, :, :], rope[1][:, :, :, :],
                                      ALU.subtract))
            own.did(api.tensor_tensor(turned[:, :, :, 1:D:2], rope[2][:, :, :, :], rope[3][:, :, :, :],
                                      ALU.add))
            own.settle(apart=True)
            if not (type(f) is int and f < 2):
                wait_apart(eng, raw_ok, 4 * (f - 1), passed)
            st = stage[par]
            own.did(api.tensor_copy(st[:, :, :, HI0:D].rearrange("p t j d -> p (t j) d"),
                                    turned[:, :, :, :].rearrange("p t j d -> p (t j) d")))
            own.did(api.tensor_copy(st[:, :, 0:J, THIRD:THIRD + D], turned[:, :, 0:J, :]))
            own.did(api.tensor_copy(st[:, :, J:2 * J, SECOND:SECOND + D], turned[:, :, J:2 * J, :]))
            own.settle()
            api.tensor_tensor(st[:, :, 0:J, SECOND:SECOND + D], turned[:, :, 0:J, :],
                              st[:, :, 0:J, HI0:D].bitcast(F32), ALU.subtract).then_inc(front_ok, 1)
            api.tensor_tensor(st[:, :, J:2 * J, THIRD:THIRD + D], turned[:, :, J:2 * J, :],
                              st[:, :, J:2 * J, HI0:D].bitcast(F32), ALU.subtract).then_inc(front_ok, 1)
            assert own.n == FRONT_STEPS

        assert SB == MB == 3 and SLOTS % 3 == 1

        def turn(par, k):
            return k + 1 + (par == 0 and k < 2)

        def lone(n, s):
            return s - (SLOTS - LEAD) if type(n) is int and n == N - 1 and s >= SLOTS - LEAD else None

        def score_bank(n, par, s):
            if lone(n, s) is not None and lone(n, s) % (SB + MB) < MB:
                return m_ps[lone(n, s) % (SB + MB)]
            return s_ps[(s + par) % SB]

        def ahead(n, par, s):
            a, m, f = has(n)
            if s < SLOTS - LEAD:
                return (n, par, s + LEAD) if a else None
            return (n + 1, 1 - par, s + LEAD - SLOTS) if m else None

        def rounds_before(n):
            if type(n) is int and n < 1:
                return sum(len(schedule(i)) for i in range(-2, n))
            if type(n) is not int or n <= N - 2:
                return rounds_before(0) + ROUNDS * n - 1
            return rounds_before(n - 1) + len(schedule(n - 1))

        def round_bank(n, r):
            return psum[r] if type(n) is int and n == -2 else shared_ps

        def schedule(n):
            a, m, f = has(n)
            out = []
            if f:
                out += [(AT_QKV[h], "qkv", h) for h in range(2)]
            if a:
                out += [(AT_SHIFT1, "shift", 1)]
            if a:
                out += [(SLOTS // 2 + 5, "out", 0)]
            if m:
                out += [(AT_SHIFT0, "shift", 0)]
            if f:
                out += [(AT_K[h], "k", h) for h in range(2)] + [(AT_Q[h], "q", h) for h in range(2)]
            if after(n):
                out += [(AT_LAST_OUT, "out", 1)]
            return [(*r, i) for i, r in enumerate(sorted(out, key=lambda r: r[0]))]

        def at(n, slot):
            return [(kind, part, rounds_before(n) + i) for s, kind, part, i in schedule(n) if s == slot]

        @block.sync
        def _(sp):
            for dst, src in ((w_all, "wqkv"), (bias, "bqkv"), (cosine, "cosine"), (sine, "sine")):
                sp.dma_start(dst[:, :, :], io[src]).then_inc(w_in if dst is w_all else const_in, 16)
            rest_v = io["rest_scratch"].rearrange("(b t p) (g f) -> p b g t f", p=P, t=KT, f=GF)
            out_v = io["out"].rearrange("b (h t p) (g f) -> p b g h t f", p=P, t=CT, f=GF)

            def body(n, par):
                a, m, f = has(n)
                if a:
                    if not (type(n) is int and n < 2):
                        wait_apart(sp, res_ok, 2 * (n - 1) + 2, passed)
                    src = rest_v[:, bass.ds(n // HG, 1), bass.ds(n % HG, 1), :, :]
                    sp.dma_start(rest[par][:, :, :], src.rearrange("p b g t f -> p (b g t) f"))\
                      .then_inc(rest_in[par], 16)
                if m:
                    wait_apart(sp, raw_ok, 4 * (n + 2), passed)
                    if a:
                        sp.wait_ge(s_full, SLOTS * n)
                    if type(n) is int and n < 1:
                        sp.wait_ge(mask_ok, 2 if n < 0 else 4)
                    for j in range(J):
                        sp.dma_start(k_mask[1 - par][j * ROWS:(j + 1) * ROWS, j, :].bitcast(F32),
                                     k_raw[1 - par][j * ROWS:(j + 1) * ROWS, :].bitcast(F32)).then_inc(kmask_in[1 - par], 16)
                    sp.dma_start(q_sh[1 - par][:, :].bitcast(F32), q_raw[1 - par][:, :].bitcast(F32))\
                      .then_inc(q_sh_in[1 - par], 16)
                if after(n):
                    store(n - 1, 1)
                if a:
                    place_shift(n, par, 1)
                    store(n, 0)
                if m:
                    place_shift(n + 1, 1 - par, 0)
                if f:
                    wait_apart(sp, raw_ok, 4 * (n + 3), passed)
                    if a:
                        sp.wait_ge(max_full, HALVES * (n + 1))
                    if type(n) is int and n < 0:
                        sp.wait_ge(mask_ok, 1 if par == 0 else 3)
                    for j in range(J):
                        rows = slice(j * ROWS, j * ROWS + SHIFT)
                        sp.dma_start(q_mask[par][rows, j, :].bitcast(F32),
                                     q_raw[par][rows, :].bitcast(F32)).then_inc(qmask_in[par], 16)


            def place_shift(m, par, h):
                wait_apart(sp, shift_t_ok, 2 * m + h + 1, passed)
                sp.wait_ge(q_sh_in[par], 16 * (m // 2 + 1))
                for j in range(J):
                    rows = slice(j * ROWS + SHIFT, j * ROWS + SHIFT + 2)
                    src = shift_t[h][j * 2 * CT:(j + 1) * 2 * CT, :].bitcast(F32)
                    sp.dma_start(q_sh[par][rows, h * CH:(h + 1) * CH].bitcast(F32),
                                 src).then_inc(shift_in[h], 16)

            def store(n, h):
                wait_apart(sp, res_ok, 2 * n + h + 1 + 2, passed)
                dst = out_v[:, bass.ds(n // HG, 1), bass.ds(n % HG, 1), h, :, :]
                sp.dma_start(dst.rearrange("p b g t f -> p (b g t) f"), result[h][:, :, :]).then_inc(res_st[h], 16)

            items(sp, body)
            for h in range(2):
                sp.wait_ge(res_st[h], 16 * (N + 1))

        @block.gpsimd
        def _(pool):
            pool.sem_inc(res_ok, 2)
            for i in range(2):
                pool.sem_inc(res_st[i], 16)
            for i in range(2):
                nc.gpsimd.memset(v_st[i][:, :, :, D:D + 1], 1.0).then_inc(v_pad_ok, 1)
                nc.gpsimd.memset(v_st[i][:, :, :, D + 1:ROWS], 0.0).then_inc(v_pad_ok, 1)
            for mask in (q_mask[0], k_mask[0]):
                nc.gpsimd.memset(mask[:, :, :].bitcast(F32), 0.0).then_inc(mask_ok, 1)
            pool.wait_ge(const_in, 48)
            pool.wait_ge(cur_ok, 2)

            def values(m, par):
                if not (type(m) is int and m < 2):
                    pool.wait_ge(pv_ok, GROUPS * (m - 1) + 2)
                wait_apart(pool, front_ok, 3 * m + 1, passed)
                nc.gpsimd.tensor_copy(v_st[par][:, :, :, 0:D].rearrange("p t j d -> p (t j) d"),
                                      v_raw[par][:, :, :, :].rearrange("p t j d -> p (t j) d")).then_inc(v_st_ok, 1)

            def combine(n, par, h, base):
                own = Chain(pool, pool_own, base, passed)
                pool.wait_ge(attn_ok, 2 * n + h + 1)
                pool.wait_ge(rest_in[par], 16 * (n // 2 + 1))
                if not (type(n) is int and n == 0):
                    pool.wait_ge(res_st[h], 16 * (n + 1))
                a_v = attn[h][:, :, :, :].rearrange("p t j d -> p t (j d)")
                gate = silu_t[:, bass.ds((n // HG) * KT + h * CT, CT), bass.ds((n % HG) * GF, GF)]
                own.did(nc.gpsimd.tensor_tensor(result[h][:, :, :], a_v, gate, ALU.mult))
                own.settle()
                nc.gpsimd.tensor_tensor(result[h][:, :, :], result[h][:, :, :],
                                        rest[par][:, h * CT:(h + 1) * CT, :], ALU.add).then_inc(res_ok, 1)

            def own_front(n):
                return has(n)[2] and not (type(n) is int and n == -2)

            def steps_of(n):
                a, m, f = has(n)
                return POOL_OUT * (after(n) + a) + FRONT_STEPS * own_front(n)

            def steps_before(n):
                if type(n) is int and n < 1:
                    return sum(steps_of(i) for i in range(-2, n))
                if type(n) is not int or n <= N - 2:
                    return steps_before(0) + POOL_STEPS * n - POOL_OUT
                return steps_before(n - 1) + steps_of(n - 1)

            def body(n, par):
                a, m, f = has(n)
                base = steps_before(n)
                if own_front(n):
                    operands(pool, nc.gpsimd, n + 2, par)
                if type(n) is int and n == -1:
                    for mask in (q_mask[1], k_mask[1]):
                        nc.gpsimd.memset(mask[:, :, :].bitcast(F32), 0.0).then_inc(mask_ok, 1)
                if after(n):
                    combine(n - 1, 1 - par, 1, base)
                    base = base + POOL_OUT
                if own_front(n):
                    front(pool, nc.gpsimd, n + 2, par, Chain(pool, pool_own, base, passed))
                    base = base + FRONT_STEPS
                if m:
                    values(n + 1, 1 - par)
                if a:
                    combine(n, par, 0, base)
                    base = base + POOL_OUT

            items(pool, body)

        @block.tensor
        def _(pe):
            pe.wait_ge(stage_ok, 5)
            pe.wait_ge(v_pad_ok, 4)
            pe.sem_inc(pv_ok, 2)

            def score(n, par, s):
                qh, kt, j = s // (KT * J), s // J % KT, s % J
                if s == 0:
                    pe.wait_ge(kmask_in[par], 16 * J * (n // 2 + 1))
                if s in (0, SLOTS // 2):
                    pe.wait_ge(shift_in[qh], 16 * J * (n + 1))
                if lone(n, s) is None:
                    pe.wait_ge(exp_ok, SLOTS * n + turn(par, s))
                elif lone(n, s) < MB:
                    pe.wait_ge(max_ok, HALVES * (n + 3) + MB)
                else:
                    pe.wait_ge(exp_ok, SLOTS * n + s + 1 - MB)
                nc.tensor.matmul(score_bank(n, par, s)[:, :], k_mask[par][:, j, kt * P:(kt + 1) * P],
                                 q_sh[par][:, qh * CH:(qh + 1) * CH], start=True, stop=True).then_inc(s_full, 1)

            def weigh(n, par, g):
                kt = g % KT
                if g == 0:
                    pe.wait_ge(v_st_ok, n + 1)
                if kt == 0:
                    pe.wait_ge(pv_out, QH * n + g // KT + 1)
                pe.wait_ge(exp_ok, SLOTS * n + J * (g + 1) + SB)
                for j in range(J):
                    last = nc.tensor.matmul(pv_ps[j * ROWS:(j + 1) * ROWS, :], v_st[par][:, kt, j, :],
                                            prob[g % 2][:, j, :], start=kt == 0, stop=kt == KT - 1)
                last.then_inc(pv_ok, 1)

            def maxima(m, par, k):
                qt, j, kh = k // 2 // J, k // 2 % J, k % 2
                if k == 0:
                    pe.wait_ge(qmask_in[par], 16 * J * (m // 2 + 1))
                    pe.wait_ge(raw_ok, 4 * (m + 1))
                pe.wait_ge(max_ok, HALVES * (m + 2) + turn(par, k))
                nc.tensor.matmul(m_ps[(k + par) % MB][:, :], q_mask[par][:, j, qt * P:(qt + 1) * P],
                                 k_raw[par][:, kh * CH:(kh + 1) * CH], start=True, stop=True).then_inc(max_full, 1)

            def rounds(n, par, slot):
                for kind, part, r in at(n, slot):
                    bank = round_bank(n, r)
                    if kind == "qkv":
                        pe.wait_ge(cur_ok, 2 * (n + 3))
                    if kind in "kq":
                        pe.wait_ge(front_ok, 3 * (n + 3))
                    if kind == "shift":
                        pe.wait_ge(shift_ok, 2 * (n + (part == 0)) + part + 1)
                    if kind == "out":
                        pe.wait_ge(pv_out, QH * (n - part) + part + 1 + 1)
                    if not (type(n) is int and n == -2):
                        pe.wait_ge(round_free, r + 1)
                    if kind == "shift":
                        nc.tensor.matmul(bank[0:J * 2 * CT, 0:P], shift[part][:, :, :, :].rearrange("p j i t -> p (j i t)"),
                                         ident_r[:, :], start=True, stop=True).then_inc(round_full, 1)
                        continue
                    for t in range(CT):
                        tile = part * CT + t
                        if kind == "qkv":
                            last = nc.tensor.matmul(bank[:, t * W:(t + 1) * W], x_cur[par][:, tile * P:(tile + 1) * P],
                                                    w_cur[par][:, :], start=True, stop=True)
                            continue
                        dst = bank[:, t * P:(t + 1) * P]
                        if kind == "out":
                            last = nc.tensor.transpose(dst, pv_sb[:, t * P:(t + 1) * P], ident[:, :])
                            continue
                        st = stage[par]
                        heads = slice(J, 2 * J) if kind == "k" else slice(0, J)
                        last = nc.tensor.matmul(dst, st[:, tile, heads, :].rearrange("p j r -> p (j r)"),
                                                ident_r[:, :], start=True, stop=True)
                    last.then_inc(round_full, 1)

            def body(n, par):
                a, m, f = has(n)
                for s in range(SLOTS):
                    if a:
                        score(n, par, s)
                    if ahead(n, par, s):
                        maxima(*ahead(n, par, s))
                    if a and s % J == 2 and s > J:
                        weigh(n, par, s // J - 1)
                    if s == 2 and after(n):
                        weigh(n - 1, 1 - par, GROUPS - 1)
                    rounds(n, par, s)

            items(pe, body)

        @block.scalar
        def _(act):
            act.sem_inc(exp_ok, SB)

            def soften(n, par, s):
                qh, kt, j = s // (KT * J), s // J % KT, s % J
                if j == 0:
                    act.wait_ge(pv_ok, GROUPS * n + s // J + 1)
                act.wait_ge(s_full, SLOTS * n + s + 1)
                nc.scalar.activation(prob[s // J % 2][:, j, :], score_bank(n, par, s)[:, :], ACT.Exp, scale=SCALE)\
                  .then_inc(exp_ok, 1)

            def rounds(n, par, slot):
                for kind, part, r in at(n, slot):
                    bank = round_bank(n, r)
                    if kind == "qkv" and part == 1:
                        act.wait_ge(pre_ok, 2 * (n + 3))
                        if not (type(n) is int and n < -1):
                            act.wait_ge(front_ok, 3 * (n + 2))
                        nc.scalar.activation(expd[:, :, :], pre[:, :, 0:2 * GF], ACT.Exp).then_inc(exp_f_ok, 1)
                    if kind == "shift":
                        m = n + (part == 0)
                        act.wait_ge(round_full, r + 1)
                        if not (type(m) is int and m == 0):
                            act.wait_ge(shift_in[part], 16 * J * m)
                        nc.scalar.activation(shift_t[part][:, :], bank[0:J * 2 * CT, 0:P], ACT.Copy).then_inc(shift_t_ok, 1)
                        act.wait_ge(shift_t_ok, 2 * m + part + 1)
                        act.sem_inc(round_free, 1)
                    if kind in ("k", "q"):
                        act.wait_ge(round_full, r + 1)
                        if kind == "k" and has(n)[0]:
                            act.wait_ge(max_full, HALVES * (n + 1))
                            act.wait_ge(kmask_in[par], 16 * J * (n // 2 + 1))
                        if kind == "q" and has(n)[0]:
                            act.wait_ge(qmask_in[par], 16 * J * (n // 2 + 1))
                            act.wait_ge(q_sh_in[par], 16 * (n // 2 + 1))
                        nc.scalar.activation({"k": k_raw, "q": q_raw}[kind][par][:, part * CH:(part + 1) * CH],
                                             bank[:, :], ACT.Copy).then_inc(raw_ok, 1)
                        act.wait_ge(raw_ok, 4 * (n + 2) + 2 * (kind == "q") + part + 1)
                        act.sem_inc(round_free, 1)

            def body(n, par):
                a, m, f = has(n)
                for s in range(SLOTS):
                    if a:
                        soften(n, par, s)
                    rounds(n, par, s)

            items(act, body)

        @block.vector
        def _(dve):
            dve.sem_inc(max_ok, 2 * HALVES + MB)
            dve.sem_inc(round_free, 1)
            dve.sem_inc(pv_out, 1)
            nc.vector.tensor_copy(ident_r[:, :], ident[:, :]).then_inc(stage_ok, 1)
            for i in range(2):
                nc.vector.memset(stage[i][:, :, 0:J, SHIFT:ROWS].bitcast(F32), 0.0).then_inc(stage_ok, 1)
                nc.vector.memset(stage[i][:, :, J:2 * J, SHIFT:SHIFT + 2].bitcast(F32), 1.0)
                nc.vector.memset(stage[i][:, :, J:2 * J, SHIFT + 2:ROWS].bitcast(F32), 0.0).then_inc(stage_ok, 1)

            operands(dve, nc.vector, 0, 0)
            dve.wait_ge(const_in, 48)

            def largest(m, par, k):
                qt, j, kh = k // 2 // J, k // 2 % J, k % 2
                dve.wait_ge(max_full, HALVES * m + k + 1)
                nc.vector.tensor_reduce(out=neg_half[par][:, qt, j, kh:kh + 1], in_=m_ps[(k + par) % MB][:, :], axis=AX.X,
                                        op=ALU.max, negate=True)\
                   .then_inc(max_ok, 1)
                if (k + 1) % (HALVES // 2) == 0:
                    h = k // (HALVES // 2)
                    ts = slice(h * CT, (h + 1) * CT)
                    dve.wait_ge(max_ok, HALVES * (m + 2) + k + 1 + MB)
                    nc.vector.tensor_tensor(neg_max[:, ts, :, :], neg_half[par][:, ts, :, 0:1],
                                            neg_half[par][:, ts, :, 1:2], ALU.min).then_inc(neg_ok, 1)
                    if not (type(m) is int and m == 0):
                        dve.wait_ge(shift_t_ok, 2 * (m - 1) + h + 1)
                    dve.wait_ge(neg_ok, 2 * m + h + 1)
                    whole = neg_max[:, ts, :, :].rearrange("p t j a -> p j (t a)")
                    hi, lo = (shift[h][:, :, i, :] for i in range(2))
                    nc.vector.tensor_copy(hi, whole).then_inc(shift_hi, 1)
                    dve.wait_ge(shift_hi, 2 * m + h + 1)
                    nc.vector.tensor_tensor(lo, whole, hi.bitcast(F32), ALU.subtract).then_inc(shift_ok, 1)

            def rounds(n, par, slot):
                for kind, part, r in at(n, slot):
                    bank = round_bank(n, r)
                    if kind == "qkv":
                        dve.wait_ge(round_full, r + 1)
                        f = n + 2
                        if part == 0 and not (type(n) is int and n < -1):
                            dve.wait_ge(front_ok, 3 * (f - 1) + 1)
                        wide = bias[:, bass.ds(f % HG, 1), :].broadcast_to([P, CT, W])
                        nc.vector.tensor_tensor(pre[:, part * CT:(part + 1) * CT, :],
                                                bank[:, 0:CT * W].rearrange("p (t w) -> p t w", w=W),
                                                wide, ALU.add).then_inc(pre_ok, 1)
                        dve.wait_ge(pre_ok, 2 * f + part + 1)
                        dve.sem_inc(round_free, 1)
                    if kind == "out":
                        dve.wait_ge(round_full, r + 1)
                        v = bank[:, :].rearrange("p (t j r) -> p t j r", t=CT, r=ROWS)
                        nc.vector.reciprocal(r_sum[:, :, :, :], v[:, :, :, D:D + 1]).then_inc(rsum_ok, 1)
                        item = n - part
                        dve.wait_ge(rsum_ok, 2 * item + part + 1)
                        dve.wait_ge(res_ok, 2 * (item - 1) + part + 1 + 2)
                        nc.vector.tensor_tensor(attn[part][:, :, :, :], v[:, :, :, 0:D],
                                                r_sum[:, :, :, :].broadcast_to([P, CT, J, D]),
                                                ALU.mult).then_inc(attn_ok, 1)
                        dve.wait_ge(attn_ok, 2 * item + part + 1)
                        dve.sem_inc(round_free, 1)

            def take_values(n, h):
                dve.wait_ge(pv_ok, GROUPS * n + (h + 1) * KT + 2)
                nc.vector.tensor_copy(pv_sb[:, :], pv_ps[:, :]).then_inc(pv_out, 1)

            def body(n, par):
                a, m, f = has(n)
                for s in range(SLOTS):
                    if ahead(n, par, s):
                        largest(*ahead(n, par, s))
                    if a and s == SLOTS // 2 + 2:
                        take_values(n, 0)
                    if s == 3 and after(n):
                        take_values(n - 1, 1)
                    rounds(n, par, s)
                if type(n) is int and n == -2:
                    front(dve, nc.vector, 0, 0, Chain(dve, dve_own, 0, passed))

            items(dve, body)


def build(nc, io):
    with ExitStack() as ctx:
        keep = {
            "ident": ctx.enter_context(nc.sbuf_tensor("ident", [P, P], F32)),
            "xnT": ctx.enter_context(nc.sbuf_tensor("xnT", [P, NTOK], F32)),
            "silu_t": ctx.enter_context(nc.sbuf_tensor("silu_t", [P, TILES, C], F32)),
        }
        io["gate_scratch"] = nc.dram_tensor("gate_scratch", [TILES * ER, P], F32).ap()
        io["rest_scratch"] = nc.dram_tensor("rest_scratch", [NTOK, C], F32).ap()
        with ExitStack() as c2:
            psum = [c2.enter_context(nc.psum_tensor(f"ps{i}", [P, 512], F32)) for i in range(8)]
            ffn = {k: c2.enter_context(nc.sbuf_tensor(k, [P, NTOK], F32R)) for k in ("xrh", "xrl")}
            ffn |= {k: c2.enter_context(nc.sbuf_tensor(k, [P, E, HID], F32R)) for k in ("w1h", "w1l", "w2h", "w2l")}
            small = {"b1": E * HT, "b2": E, "wv": C, "cols": 5}
            ffn |= {k: c2.enter_context(nc.sbuf_tensor(k, [P, n], F32)) for k, n in small.items()}
            prologue(nc, keep, ffn, io, psum)
            experts(nc, keep, ffn, io, psum)
        with ExitStack() as c3:
            psum = [c3.enter_context(nc.psum_tensor(f"pa{i}", [P, 512], F32)) for i in range(8)]
            attention(nc, keep, io, psum)


def kernel(**inputs):
    import numpy as np
    import concourse.bacc as bacc
    from concourse.bass_utils import run_bass_kernel_spmd

    a = {k[3:]: np.asarray(v) for k, v in inputs.items()}
    w = a["attn_w_qkv"].reshape(3, HG, GF, C)
    bq = a["attn_b_qkv"].reshape(3, HG, GF)

    def lay(x):
        return np.ascontiguousarray(x)

    w1 = np.concatenate([a["ffn_W1_s"], a["ffn_W1_r"]])
    w2 = np.concatenate([a["ffn_W2_s"], a["ffn_W2_r"]])
    b1 = np.concatenate([a["ffn_b1_s"], a["ffn_b1_r"]])
    b2 = np.concatenate([a["ffn_b2_s"], a["ffn_b2_r"]])
    pos = np.arange(T, dtype=np.float32)[:, None]
    div = np.exp(np.arange(0, D, 2, dtype=np.float32) * np.float32(-np.log(10000.0) / D)).astype(np.float32)
    ang = pos * div
    def table(f):
        return lay(f(ang).astype(np.float32).reshape(BT, P, D // 2).transpose(1, 0, 2))

    arrays = {
        "x": lay(a["attn_x"]),
        "ident": np.eye(P, dtype=np.float32),
        "rank": lay(np.broadcast_to(np.arange(ER, 0, -1, dtype=np.float32), (P, TILES, ER))),
        "cosine": table(np.cos),
        "sine": table(np.sin),
        "cent": lay(a["ffn_centroids"]),
        "gains": lay(np.stack([a["ffn_g_shared"]] * ES + [a["ffn_g_routed"]] * ER, axis=1)),
        "w1": lay(w1.transpose(1, 0, 2)),
        "w2": lay(w2.reshape(E, HT, P, C).transpose(2, 0, 1, 3).reshape(P, E, HID)),
        "b1": lay(b1.reshape(E * HT, P).T),
        "b2": lay(b2.T),
        "wv": lay(w[2].reshape(C, C).T),
        "cols": lay(np.concatenate([a["attn_w_lepe"][:, 0, :], a["attn_b_lepe"][:, None],
                                    a["attn_b_qkv"][2 * C:, None]], axis=1)),
        "wqkv": lay(w.transpose(3, 1, 0, 2).reshape(C, HG, 3 * GF)),
        "bqkv": lay(np.broadcast_to(bq.transpose(1, 0, 2).reshape(1, HG, 3 * GF), (P, HG, 3 * GF))),
    }
    nc = bacc.Bacc("TRN2", target_bir_lowering=False, num_devices=1)
    io = {k: nc.dram_tensor(f"in_{k}", v.shape, mybir.dt.from_np(v.dtype), kind="ExternalInput").ap()
          for k, v in arrays.items()}
    io["out"] = nc.dram_tensor("out", (B, T, C), F32, kind="ExternalOutput").ap()
    build(nc, io)
    r = run_bass_kernel_spmd(nc, [{f"in_{k}": v for k, v in arrays.items()}], core_ids=[0])
    return r.results[0]["out"]
```
